# Optimizing a Trainium2 kernel written in Bass

```python
import numpy as np
import jax
import jax.numpy as jnp

def _softmax(x, axis=-1):
    return jax.nn.softmax(x, axis=axis)

def _gelu(x):
    return jax.nn.gelu(x, approximate=True)

def _silu(x):
    return jax.nn.silu(x)

def _sigmoid(x):
    return jax.nn.sigmoid(x)

def _layernorm(x, axis=-1, eps=1e-05):
    m = jnp.mean(x, axis=axis, keepdims=True)
    v = jnp.var(x, axis=axis, keepdims=True)
    return (x - m) / jnp.sqrt(v + eps)

def _scatter_add(tgt, idx, src, axis=0):
    return tgt.at[idx].add(src)

def _segment_sum(src, seg, n):
    return jax.ops.segment_sum(src, seg, n)
kernel_name = 'mk_dlrm_tower_d1_rec_r8_a581c6'

def setup_inputs(seed: int=0):
    np.random.seed(seed)
    _w = jnp.asarray

    def _rec_inputs():
        import jax
        import jax.numpy as jnp
        _tk = jax.random.key(seed)
        ids = jnp.stack([jax.random.randint(jax.random.fold_in(_tk, 200 + f), (2048,), 0, v, jnp.int32) for f, v in enumerate([1250, 125000, 12500, 1250, 1000, 1250, 1250, 12500, 1250, 1000, 1250, 1000, 1000, 12500, 1000, 1250, 1250, 12500, 12500, 1250, 1000, 1000, 1250, 12500, 12500, 1000])], axis=1)
        tbl_0 = 0.05 * jax.random.normal(jax.random.fold_in(_tk, 500 + 0), (1250, 128), jnp.float32)
        tbl_1 = 0.05 * jax.random.normal(jax.random.fold_in(_tk, 500 + 1), (125000, 128), jnp.float32)
        tbl_2 = 0.05 * jax.random.normal(jax.random.fold_in(_tk, 500 + 2), (12500, 128), jnp.float32)
        tbl_3 = 0.05 * jax.random.normal(jax.random.fold_in(_tk, 500 + 3), (1250, 128), jnp.float32)
        tbl_4 = 0.05 * jax.random.normal(jax.random.fold_in(_tk, 500 + 4), (1000, 128), jnp.float32)
        tbl_5 = 0.05 * jax.random.normal(jax.random.fold_in(_tk, 500 + 5), (1250, 128), jnp.float32)
        tbl_6 = 0.05 * jax.random.normal(jax.random.fold_in(_tk, 500 + 6), (1250, 128), jnp.float32)
        tbl_7 = 0.05 * jax.random.normal(jax.random.fold_in(_tk, 500 + 7), (12500, 128), jnp.float32)
        tbl_8 = 0.05 * jax.random.normal(jax.random.fold_in(_tk, 500 + 8), (1250, 128), jnp.float32)
        tbl_9 = 0.05 * jax.random.normal(jax.random.fold_in(_tk, 500 + 9), (1000, 128), jnp.float32)
        tbl_10 = 0.05 * jax.random.normal(jax.random.fold_in(_tk, 500 + 10), (1250, 128), jnp.float32)
        tbl_11 = 0.05 * jax.random.normal(jax.random.fold_in(_tk, 500 + 11), (1000, 128), jnp.float32)
        tbl_12 = 0.05 * jax.random.normal(jax.random.fold_in(_tk, 500 + 12), (1000, 128), jnp.float32)
        tbl_13 = 0.05 * jax.random.normal(jax.random.fold_in(_tk, 500 + 13), (12500, 128), jnp.float32)
        tbl_14 = 0.05 * jax.random.normal(jax.random.fold_in(_tk, 500 + 14), (1000, 128), jnp.float32)
        tbl_15 = 0.05 * jax.random.normal(jax.random.fold_in(_tk, 500 + 15), (1250, 128), jnp.float32)
        tbl_16 = 0.05 * jax.random.normal(jax.random.fold_in(_tk, 500 + 16), (1250, 128), jnp.float32)
        tbl_17 = 0.05 * jax.random.normal(jax.random.fold_in(_tk, 500 + 17), (12500, 128), jnp.float32)
        tbl_18 = 0.05 * jax.random.normal(jax.random.fold_in(_tk, 500 + 18), (12500, 128), jnp.float32)
        tbl_19 = 0.05 * jax.random.normal(jax.random.fold_in(_tk, 500 + 19), (1250, 128), jnp.float32)
        tbl_20 = 0.05 * jax.random.normal(jax.random.fold_in(_tk, 500 + 20), (1000, 128), jnp.float32)
        tbl_21 = 0.05 * jax.random.normal(jax.random.fold_in(_tk, 500 + 21), (1000, 128), jnp.float32)
        tbl_22 = 0.05 * jax.random.normal(jax.random.fold_in(_tk, 500 + 22), (1250, 128), jnp.float32)
        tbl_23 = 0.05 * jax.random.normal(jax.random.fold_in(_tk, 500 + 23), (12500, 128), jnp.float32)
        tbl_24 = 0.05 * jax.random.normal(jax.random.fold_in(_tk, 500 + 24), (12500, 128), jnp.float32)
        tbl_25 = 0.05 * jax.random.normal(jax.random.fold_in(_tk, 500 + 25), (1000, 128), jnp.float32)
        _rk = jax.random.fold_in(_tk, 7)
        r_dense_features = -0.000520686 + 1.00062 * jax.random.normal(jax.random.fold_in(_rk, 101), (2048, 128), jnp.float32)
        W_top1 = 0.0405887 * jax.random.normal(jax.random.fold_in(_tk, 801), (607, 512), jnp.float32)
        W_top2 = 0.0441942 * jax.random.normal(jax.random.fold_in(_tk, 802), (512, 256), jnp.float32)
        W_top3 = 0.0625 * jax.random.normal(jax.random.fold_in(_tk, 803), (256, 1), jnp.float32)
        b_top1 = jnp.zeros((512,), jnp.float32)
        b_top2 = jnp.zeros((256,), jnp.float32)
        return (r_dense_features, ids, tbl_0, tbl_1, tbl_2, tbl_3, tbl_4, tbl_5, tbl_6, tbl_7, tbl_8, tbl_9, tbl_10, tbl_11, tbl_12, tbl_13, tbl_14, tbl_15, tbl_16, tbl_17, tbl_18, tbl_19, tbl_20, tbl_21, tbl_22, tbl_23, tbl_24, tbl_25, W_top1, b_top1, W_top2, b_top2, W_top3)
    r_dense_features, ids, tbl_0, tbl_1, tbl_2, tbl_3, tbl_4, tbl_5, tbl_6, tbl_7, tbl_8, tbl_9, tbl_10, tbl_11, tbl_12, tbl_13, tbl_14, tbl_15, tbl_16, tbl_17, tbl_18, tbl_19, tbl_20, tbl_21, tbl_22, tbl_23, tbl_24, tbl_25, W_top1, b_top1, W_top2, b_top2, W_top3 = _rec_inputs()

    def _L0_rec_setup():
        import jax, jax.numpy as jnp
        import numpy as np
        F = 26
        N = F + 1
        _TRIU_I, _TRIU_J = np.triu_indices(N, k=1)
        key = jax.random.key(seed)
        k1, k2 = jax.random.split(key)
        B, D = (2048, 128)
        dense_features = jax.random.normal(k1, (B, D), dtype=jnp.float32)
        sparse_features = jax.random.normal(k2, (B, F, D), dtype=jnp.float32)
        return {'dense_features': dense_features, 'sparse_features': sparse_features}
    _L0_rec_all = _L0_rec_setup()
    _L0_rec_in = {k: v for k, v in _L0_rec_all.items() if k in ()}
    del _L0_rec_all
    return {'r_dense_features': r_dense_features, 'ids': ids, 'tbl_0': tbl_0, 'tbl_1': tbl_1, 'tbl_2': tbl_2, 'tbl_3': tbl_3, 'tbl_4': tbl_4, 'tbl_5': tbl_5, 'tbl_6': tbl_6, 'tbl_7': tbl_7, 'tbl_8': tbl_8, 'tbl_9': tbl_9, 'tbl_10': tbl_10, 'tbl_11': tbl_11, 'tbl_12': tbl_12, 'tbl_13': tbl_13, 'tbl_14': tbl_14, 'tbl_15': tbl_15, 'tbl_16': tbl_16, 'tbl_17': tbl_17, 'tbl_18': tbl_18, 'tbl_19': tbl_19, 'tbl_20': tbl_20, 'tbl_21': tbl_21, 'tbl_22': tbl_22, 'tbl_23': tbl_23, 'tbl_24': tbl_24, 'tbl_25': tbl_25, 'W_top1': W_top1, 'b_top1': b_top1, 'W_top2': W_top2, 'b_top2': b_top2, 'W_top3': W_top3}

def reference(r_dense_features, ids, tbl_0, tbl_1, tbl_2, tbl_3, tbl_4, tbl_5, tbl_6, tbl_7, tbl_8, tbl_9, tbl_10, tbl_11, tbl_12, tbl_13, tbl_14, tbl_15, tbl_16, tbl_17, tbl_18, tbl_19, tbl_20, tbl_21, tbl_22, tbl_23, tbl_24, tbl_25, W_top1, b_top1, W_top2, b_top2, W_top3):
    import jax
    import jax.numpy as jnp

    def _L0_rec_ref(dense_features, sparse_features):
        import jax, jax.numpy as jnp
        import numpy as np
        F = 26
        N = F + 1
        _TRIU_I, _TRIU_J = np.triu_indices(N, k=1)
        combined = jnp.concatenate([dense_features[:, None, :], sparse_features], axis=1)
        interactions = jnp.einsum('bnd,bmd->bnm', combined, combined)
        interactions_flat = interactions[:, _TRIU_I, _TRIU_J]
        return jnp.concatenate([dense_features, interactions_flat], axis=1)
    e = jnp.stack([tbl_0[ids[:, 0]], tbl_1[ids[:, 1]], tbl_2[ids[:, 2]], tbl_3[ids[:, 3]], tbl_4[ids[:, 4]], tbl_5[ids[:, 5]], tbl_6[ids[:, 6]], tbl_7[ids[:, 7]], tbl_8[ids[:, 8]], tbl_9[ids[:, 9]], tbl_10[ids[:, 10]], tbl_11[ids[:, 11]], tbl_12[ids[:, 12]], tbl_13[ids[:, 13]], tbl_14[ids[:, 14]], tbl_15[ids[:, 15]], tbl_16[ids[:, 16]], tbl_17[ids[:, 17]], tbl_18[ids[:, 18]], tbl_19[ids[:, 19]], tbl_20[ids[:, 20]], tbl_21[ids[:, 21]], tbl_22[ids[:, 22]], tbl_23[ids[:, 23]], tbl_24[ids[:, 24]], tbl_25[ids[:, 25]]], axis=1)
    z = _L0_rec_ref(r_dense_features, e)
    z = z.reshape(z.shape[0], -1)
    h = jnp.concatenate([z, r_dense_features], axis=1)
    h = jnp.maximum(h @ W_top1 + b_top1, 0.0)
    h = jnp.maximum(h @ W_top2 + b_top2, 0.0)
    y = h @ W_top3
    return y

_drawn_inputs = setup_inputs


def setup_inputs(seed=0):
    import zlib

    import numpy as np

    out = dict(_drawn_inputs(seed))
    spreads = {'b_top1': (0.0, 0.1), 'b_top2': (0.0, 0.1)}
    factors = {}
    for name, (base, spread) in spreads.items():
        noise = np.random.default_rng([zlib.crc32(name.encode()), seed]).standard_normal(out[name].shape)
        drawn = base * np.exp(spread * noise) if base else spread * noise
        out[name] = jnp.asarray(drawn.astype(out[name].dtype))
    for name, factor in factors.items():
        out[name] = (out[name] * factor).astype(out[name].dtype)
    return out
```

```python
from contextlib import ExitStack

import concourse.bass as bass
from concourse import mybir

BATCH, DIM = 2048, 128
ROWS = (1250, 125000, 12500, 1250, 1000, 1250, 1250, 12500, 1250, 1000, 1250, 1000, 1000, 12500, 1000, 1250,
        1250, 12500, 12500, 1250, 1000, 1000, 1250, 12500, 12500, 1000)
FIELDS = len(ROWS)
SHORT = 1000
GATHERED = [f for f in range(FIELDS) if ROWS[f] != SHORT]
ONE_HOT = [f for f in range(FIELDS) if ROWS[f] == SHORT]
PARTS = 8
PART_ROWS = SHORT // PARTS
VECTORS = FIELDS + 1
TRANSPOSED = 1 + len(GATHERED)
PAIRS = VECTORS * (VECTORS - 1) // 2
DELTAS = VECTORS // 2
PAD = 32
TILE = 128
TILES = 2
CHUNK = TILES * TILE
CHUNKS = BATCH // CHUNK
QUADS = 4
GROUPS = TILE // QUADS
CHUNK_GROUPS = CHUNK // QUADS
BANK = 512
BATCH_VECTORS = BANK // TILE
BATCHES = -(-TRANSPOSED // BATCH_VECTORS)
HOT_FIELDS = BANK // CHUNK
HOT_BATCHES = -(-len(ONE_HOT) // HOT_FIELDS)
LAYER = 5
HOT_BUFFERS = 4
BANK_GROUPS = 4
STEP_GROUPS = 2 * BANK_GROUPS
STEPS = GROUPS // STEP_GROUPS
STEP_FIELDS = 2 * BANK // CHUNK
INDEX_STEPS = len(ONE_HOT) // STEP_FIELDS
HIDDEN1, HIDDEN2 = 512, 256
PAIR_TILES = 3
PAIR_ROWS = PAIRS // PAIR_TILES
KTILES = PAIR_TILES + 1
MTILES1, MTILES2 = HIDDEN1 // 128, HIDDEN2 // 128
TILE0_AFTER = (1, 3, 4, 5, 6)
IN_LAYERS = ((0,), (1,), (2,), (3,), (4,))
IN_PRODUCTS = ((0,), (1, 2), (3, 4), ())
STAGES = 4

WRAP = VECTORS + DELTAS - 1
SLOT = QUADS * CHUNK_GROUPS
SLOTS = VECTORS * WRAP + (VECTORS + 1) * (VECTORS - 1) + 1
FIRST_SLOT = VECTORS * (WRAP - DELTAS)


def batch_vectors(b):
    return range(b * BATCH_VECTORS, min((b + 1) * BATCH_VECTORS, TRANSPOSED))


def build(nc, dense, ids, tables, w1, b1, w2, b2, w3, out):
    fp32, fp32r, fp16, int32 = mybir.dt.float32, mybir.dt.float32r, mybir.dt.float16, mybir.dt.int32
    ALU, ACT = mybir.AluOpType, mybir.ActivationFunctionType

    scratch = nc.dram_tensor("scratch", (SLOTS, QUADS, CHUNK_GROUPS), fp32, kind="Internal").ap()

    with ExitStack() as ctx:
        def sb(name, shape, dt=fp32):
            return ctx.enter_context(nc.sbuf_tensor(name, shape, dt))

        def ps(name, shape):
            return ctx.enter_context(nc.psum_tensor(name, shape, fp32))

        def sem(name):
            return ctx.enter_context(nc.semaphore(name))

        identity = sb("identity", [128, 128])
        identity16 = sb("identity16", [128, 128], fp16)
        row_of_int = sb("row_of_int", [128, PARTS], int32)
        row_of = sb("row_of", [128, PARTS])
        ids_sb = sb("ids_sb", [TILE, BATCH // TILE, FIELDS], int32)
        index = [sb(f"index{t}", [TILE, FIELDS], int32) for t in range(TILES)]
        hot_ids = sb("hot_ids", [TILE, TILES, len(ONE_HOT)], fp16)
        hot_ids_all = sb("hot_ids_all", [128, len(ONE_HOT), CHUNK])
        one_hot = sb("one_hot", [PART_ROWS, HOT_BUFFERS, PARTS, CHUNK], fp32r)
        high = sb("high", [PART_ROWS, len(ONE_HOT), PARTS, DIM], fp32r)
        low = sb("low", [PART_ROWS, len(ONE_HOT), PARTS, DIM], fp32r)
        rows = [sb(f"rows{t}", [TILE, TRANSPOSED, DIM]) for t in range(TILES)]
        vectors = sb("vectors", [DIM, CHUNK, PAD])
        products = sb("products", [128, VECTORS, CHUNK_GROUPS])
        features = sb("features", [128, KTILES, CHUNK])
        w1_sb = sb("w1_sb", [128, KTILES, HIDDEN1])
        w1_again = sb("w1_again", [128, HIDDEN1])
        w2_sb = sb("w2_sb", [128, MTILES1, HIDDEN2])
        w3_sb = sb("w3_sb", [128, MTILES2])
        b1_sb = sb("b1_sb", [128, MTILES1])
        b2_sb = sb("b2_sb", [128, MTILES2])
        hidden1 = sb("hidden1", [128, MTILES1, CHUNK])
        hidden2 = sb("hidden2", [128, MTILES2, CHUNK])
        y_sb = sb("y_sb", [1, BATCH])
        stage = [sb(f"stage{n}", [128, PARTS, DIM]) for n in range(2)] + [
            x[:, :, :].rearrange("p k (h d) -> p (k h) d", d=DIM) for x in (features, hidden1)]

        moved = ps("moved", [128, 2, BANK])
        gram = ps("gram", [128, 2, 2, BANK])
        mlp = ps("mlp", [128, 2, 2, CHUNK])

        ids_loaded = sem("ids_loaded")
        dense_loaded = [sem(f"dense_loaded{t}") for t in range(TILES)]
        table_loaded = [sem(f"table_loaded{n}") for n in range(STAGES)]
        weights_loaded = sem("weights_loaded")
        constants_made = sem("constants_made")
        identity16_made = sem("identity16_made")
        index_ready = [sem(f"index_ready{t}") for t in range(TILES)]
        hot_ids_ready = sem("hot_ids_ready")
        rows_loaded = [[sem(f"rows_loaded{t}_{b}") for b in range(BATCHES)] for t in range(TILES)]
        high_made = sem("high_made")
        low_made = sem("low_made")
        rows_numbered = sem("rows_numbered")
        weights_summed = sem("weights_summed")
        dense_kept = sem("dense_kept")
        one_hot_made = sem("one_hot_made")
        batch_ready = sem("batch_ready")
        batch_kept = sem("batch_kept")
        hot_ready = sem("hot_ready")
        hot_kept = sem("hot_kept")
        step_ready = sem("step_ready")
        step_kept = sem("step_kept")
        scratch_written = sem("scratch_written")
        pairs_loaded = sem("pairs_loaded")
        layer_ready = sem("layer_ready")
        layer_kept = sem("layer_kept")
        out_written = sem("out_written")

        CHUNK_BATCHES = TILES * BATCHES
        CHUNK_STEPS = TILES * STEPS + INDEX_STEPS
        assert CHUNK_BATCHES % 2 == CHUNK_STEPS % 2 == HOT_BATCHES % 2 == INDEX_STEPS % 2 == 0
        SCRATCH_DMAS = 2 * QUADS
        WEIGHTS = 7
        CONSTANTS = 5

        def tile_step(t, s, last):
            return (1 if last else 2) * INDEX_STEPS + t * STEPS + s

        def chunks(engine, chunk):
            chunk(0, True, False)
            with engine.Fori(1, CHUNKS - 1) as c:
                chunk(c, False, False)
            chunk(CHUNKS - 1, False, True)

        block = ctx.enter_context(nc.Block())

        @block.sync
        def _(sp):
            def load_dense(at, t):
                sp.dma_start(rows[t][:, 0, :], dense[bass.ds(at, TILE), :]).then_inc(dense_loaded[t], 16)

            def load_table(n):
                sp.dma_start(stage[n % STAGES][0:PART_ROWS, :, :],
                             tables[ONE_HOT[n]].rearrange("(p k) d -> p k d", k=PARTS))\
                    .then_inc(table_loaded[n % STAGES], 16)

            sp.dma_start(ids_sb[:, :, :], ids.rearrange("(t p) f -> p t f", p=TILE)).then_inc(ids_loaded, 16)
            for n in range(STAGES):
                load_table(n)
            for t in range(TILES):
                load_dense(t * TILE, t)
            for n in range(STAGES, len(ONE_HOT)):
                sp.wait_ge(low_made, n - STAGES + 1)
                load_table(n)
            for into, source in (
                (w1_sb[0:PAIR_ROWS, 0:PAIR_TILES, :], w1[0:PAIRS, :].rearrange("(k p) n -> p k n", p=PAIR_ROWS)),
                (w1_sb[:, PAIR_TILES, :], w1[PAIRS:PAIRS + DIM, :]),
                (w1_again[:, :], w1[PAIRS + DIM:PAIRS + 2 * DIM, :]),
                (w2_sb[:, :, :], w2.rearrange("(k p) n -> p k n", p=128)),
                (w3_sb[:, :], w3),
                (b1_sb[:, :], b1),
                (b2_sb[:, :], b2),
            ):
                sp.dma_start(into, source).then_inc(weights_loaded, 16)

            def chunk(c, first, last):
                if not first:
                    sp.wait_ge(pairs_loaded, c * 16)
                if not last:
                    for t in range(TILES):
                        at = c * CHUNK + (CHUNK + t * TILE)
                        if not first:
                            at = sp.snap(at)
                        sp.wait_ge(batch_ready, c * CHUNK_BATCHES + (t * BATCHES + 1))
                        load_dense(at, t)
                sp.wait_ge(step_kept, c * CHUNK_STEPS + (2 + tile_step(1, STEPS, last)))
                for q in range(QUADS):
                    part = slice(PAD * q, PAD * q + VECTORS)
                    for first_column, slot in ((0, VECTORS * (WRAP - VECTORS + 1)), (VECTORS - DELTAS, 0)):
                        into = bass.AP(scratch.tensor, slot * SLOT + q * CHUNK_GROUPS,
                                       [[(VECTORS + 1) * SLOT, VECTORS], [VECTORS * SLOT, VECTORS - first_column],
                                        [1, CHUNK_GROUPS]])
                        sp.dma_start(into, products[part, first_column:VECTORS, :]).then_inc(scratch_written, 16)
                if not first:
                    sp.wait_ge(layer_ready, c * LAYER + (2 - LAYER))
                sp.wait_ge(scratch_written, c * (16 * SCRATCH_DMAS) + 16 * SCRATCH_DMAS)
                sp.dma_start(features[0:PAIR_ROWS, 0:PAIR_TILES, :],
                             scratch[FIRST_SLOT:FIRST_SLOT + PAIRS, :, :]
                             .rearrange("(k p) q g -> p k (q g)", p=PAIR_ROWS)).then_inc(pairs_loaded, 16)

            chunks(sp, chunk)
            sp.wait_ge(layer_kept, LAYER * CHUNKS)
            sp.dma_start(out.rearrange("b o -> o b"), y_sb[:, :]).then_inc(out_written, 16)
            sp.wait_ge(out_written, 16)

        @block.gpsimd
        def _(pool):
            nc.gpsimd.memset(identity[:, :], 0.0).then_inc(constants_made, 1)
            nc.gpsimd.iota(row_of_int[:, :], pattern=[[1, PARTS]], base=0, channel_multiplier=PARTS)\
                .then_inc(constants_made, 1)
            nc.gpsimd.memset(vectors[:, 0:TILE, VECTORS:PAD], 0.0).then_inc(constants_made, 1)
            nc.gpsimd.memset(vectors[:, TILE:CHUNK, VECTORS:PAD], 0.0).then_inc(constants_made, 1)
            pool.wait_ge(constants_made, CONSTANTS - 1)
            nc.gpsimd.affine_select(out=identity[:, :], in_=identity[:, :], compare_op=ALU.not_equal, fill=1.0,
                                    base=0, pattern=[[-1, 128]], channel_multiplier=1).then_inc(constants_made, 1)

            def gather(t, b):
                for v in batch_vectors(b):
                    if v:
                        f = GATHERED[v - 1]
                        pool.indirect_dma_start(
                            rows[t][:, v, :], None, tables[f][:, :],
                            bass.IndirectOffsetOnAxis(ap=index[t][:, f:f + 1], axis=0),
                        ).then_inc(rows_loaded[t][b], 16)

            for t in range(TILES):
                pool.wait_ge(index_ready[t], 1)
                for b in range(BATCHES):
                    gather(t, b)
            batches = pool.alloc_register("batches")
            pool.reg_mov(batches, 1)
            with pool.Fori(1, CHUNKS) as c:
                for t in range(TILES):
                    for b in range(BATCHES):
                        count = pool.snap(batches)
                        if b == 0:
                            pool.wait_ge(index_ready[t], c + 1)
                        pool.wait_ge(batch_ready, count)
                        pool.reg_add(batches, batches, 1)
                        gather(t, b)

        @block.tensor
        def _(pe):
            def transpose_batch(c, t, b):
                n = t * BATCHES + b
                batch = batch_vectors(b)
                gathers = len(batch) - (b == 0)
                pe.wait_ge(rows_loaded[t][b], c * (16 * gathers) + 16 * gathers)
                if b == 0:
                    pe.wait_ge(dense_loaded[t], c * 16 + 16)
                pe.wait_ge(batch_kept, c * CHUNK_BATCHES + (n + 1))
                for m, v in enumerate(batch):
                    last = nc.tensor.transpose(moved[:, n % 2, m * TILE:(m + 1) * TILE], rows[t][:, v, :],
                                               identity[:, :])
                last.then_inc(batch_ready, 1)

            def multiply(c, t, last_chunk, between=lambda s: None):
                pe.wait_ge(batch_kept, c * CHUNK_BATCHES + (2 + (t + 1) * BATCHES))
                if t == 0:
                    pe.wait_ge(hot_kept, c * HOT_BATCHES + (2 + HOT_BATCHES))
                for s in range(STEPS):
                    n = tile_step(t, s, last_chunk)
                    pe.wait_ge(step_kept, c * CHUNK_STEPS + (n + 1))
                    for g in range(STEP_GROUPS):
                        at = t * TILE + (s * STEP_GROUPS + g) * QUADS
                        bank, col = divmod(g, BANK_GROUPS)
                        col *= QUADS * VECTORS
                        four = vectors[:, at:at + QUADS, :]
                        last = nc.tensor.matmul(gram[:, n % 2, bank, col:col + QUADS * VECTORS],
                                                four.rearrange("d s v -> d (s v)"), four[:, :, 0:VECTORS],
                                                start=True, stop=True)
                    last.then_inc(step_ready, 1)
                    between(s)

            def broadcast_indices(c, step0):
                pe.wait_ge(hot_ids_ready, c + 1)
                for s in range(INDEX_STEPS):
                    n = step0 + s
                    pe.wait_ge(step_kept, n + 1)
                    for m in range(STEP_FIELDS):
                        h = s * STEP_FIELDS + m
                        bank, col = divmod(m * CHUNK, BANK)
                        for t in range(TILES):
                            last = nc.tensor.matmul(gram[:, s % 2, bank, col + t * TILE:col + (t + 1) * TILE],
                                                    hot_ids[:, t, h:h + 1].broadcast_to([TILE, 128]),
                                                    identity16[:, :], start=True, stop=True)
                    last.then_inc(step_ready, 1)

            def look_up(c, h, first_chunk):
                j, m = divmod(h, HOT_FIELDS)
                if first_chunk:
                    pe.wait_ge(low_made, h + 1)
                if m == 0:
                    pe.wait_ge(hot_kept, c * HOT_BATCHES + (j + 1))
                pe.wait_ge(one_hot_made, c * len(ONE_HOT) + (h + 1))
                for part in (high, low):
                    for k in range(PARTS):
                        last = nc.tensor.matmul(mlp[:, j % 2, m, :], part[:, h, k, :],
                                                one_hot[:, h % HOT_BUFFERS, k, :],
                                                start=(part is high and k == 0),
                                                stop=(part is low and k == PARTS - 1))
                if m == HOT_FIELDS - 1:
                    last.then_inc(hot_ready, 1)

            def layers(c, between, lookups):
                pe.wait_ge(pairs_loaded, c * 16 + 16)
                pe.wait_ge(dense_kept, c + 1)
                if lookups is None:
                    pe.wait_ge(layer_kept, c * LAYER)
                for m in range(MTILES1):
                    if m % 2 == 0 and lookups is not None:
                        pe.wait_ge(hot_kept, lookups * HOT_BATCHES + (2 + HOT_BATCHES - 1 + m // 2))
                    for k in range(KTILES):
                        height = PAIR_ROWS if k < PAIR_TILES else DIM
                        last = nc.tensor.matmul(mlp[:, m // 2, m % 2, :],
                                                w1_sb[0:height, k, m * 128:(m + 1) * 128],
                                                features[0:height, k, :], start=(k == 0), stop=(k == KTILES - 1))
                    if m % 2:
                        last.then_inc(layer_ready, 1)
                    between(m)
                for m in range(MTILES2):
                    for k in range(MTILES1):
                        if m == 0 and k % 2 == 0:
                            pe.wait_ge(layer_kept, c * LAYER + (1 + k // 2))
                        last = nc.tensor.matmul(mlp[:, m, 0, :], w2_sb[:, k, m * 128:(m + 1) * 128],
                                                hidden1[:, k, :], start=(k == 0), stop=(k == MTILES1 - 1))
                    last.then_inc(layer_ready, 1)
                between(4)
                for k in range(MTILES2):
                    pe.wait_ge(layer_kept, c * LAYER + (3 + k))
                    last = nc.tensor.matmul(mlp[0:1, 0, 1, :], w3_sb[:, k:k + 1], hidden2[:, k, :],
                                            start=(k == 0), stop=(k == MTILES2 - 1))
                last.then_inc(layer_ready, 1)

            def chunk(c, first, last):
                for h in range(len(ONE_HOT)):
                    look_up(c, h, first)
                    if h in TILE0_AFTER:
                        transpose_batch(c, 0, TILE0_AFTER.index(h))
                if not last:
                    broadcast_indices(c + 1, c * CHUNK_STEPS + INDEX_STEPS)
                if first:
                    pe.wait_ge(weights_summed, 1)
                    multiply(c, 0, last)
                    for b in range(BATCHES):
                        transpose_batch(c, 1, b)
                elif not last:
                    layers(c - 1, lambda n: [transpose_batch(c, 1, b) for b in IN_LAYERS[n]], c)
                    multiply(c, 0, last)
                else:
                    multiply(c, 0, last, lambda s: [transpose_batch(c, 1, b) for b in IN_PRODUCTS[s]])
                multiply(c, 1, last)
                if last:
                    layers(c - 1, lambda n: None, None)

            pe.wait_ge(identity16_made, 1)
            broadcast_indices(0, 0)
            chunks(pe, chunk)
            layers(CHUNKS - 1, lambda n: None, None)

        @block.vector
        def _(dve):
            def ready_index(tile, t):
                nc.vector.tensor_copy(index[t][:, :], ids_sb[:, tile, :]).then_inc(index_ready[t], 1)

            def ready_hot_ids(tiles):
                runs = []
                for h, f in enumerate(ONE_HOT):
                    if runs and ONE_HOT[runs[-1][0]] + runs[-1][1] == f:
                        runs[-1][1] += 1
                    else:
                        runs.append([h, 1])
                for h, count in runs:
                    last = nc.vector.tensor_copy(hot_ids[:, :, h:h + count],
                                                 ids_sb[:, tiles, ONE_HOT[h]:ONE_HOT[h] + count])
                last.then_inc(hot_ids_ready, 1)

            def make_one_hot(h):
                for k in range(PARTS):
                    last = nc.vector.tensor_scalar(one_hot[:, h % HOT_BUFFERS, k, :], hot_ids_all[0:PART_ROWS, h, :],
                                                   row_of[0:PART_ROWS, k:k + 1], None, ALU.is_equal)
                last.then_inc(one_hot_made, 1)

            def keep_lookups(c, and_then):
                made = HOT_BUFFERS
                for j in range(HOT_BATCHES):
                    if j == HOT_BATCHES - 1:
                        and_then()
                    dve.wait_ge(hot_ready, c * HOT_BATCHES + (j + 1))
                    v = TRANSPOSED + j * HOT_FIELDS
                    nc.vector.tensor_copy(vectors[:, :, v:v + HOT_FIELDS].rearrange("d s v -> d v s"),
                                          mlp[:, j % 2, :, :]).then_inc(hot_kept, 1)
                    for _ in range(HOT_FIELDS):
                        if made < len(ONE_HOT):
                            make_one_hot(made)
                            made += 1

            def split(h):
                dve.wait_ge(high_made, h + 1)
                nc.vector.tensor_tensor(low[:, h, :, :], stage[h % STAGES][0:PART_ROWS, :, :],
                                        high[:, h, :, :].bitcast(fp32), ALU.subtract).then_inc(low_made, 1)

            dve.sem_inc(hot_kept, 2)
            dve.wait_ge(ids_loaded, 16)
            for t in range(TILES):
                ready_index(t, t)
            ready_hot_ids(slice(0, TILES))
            dve.wait_ge(constants_made, CONSTANTS)
            nc.vector.tensor_copy(row_of[:, :], row_of_int[:, :]).then_inc(rows_numbered, 1)
            nc.vector.tensor_copy(identity16[:, :], identity[:, :]).then_inc(identity16_made, 1)
            dve.wait_ge(rows_numbered, 1)
            for h in range(HOT_BUFFERS):
                split(h)
                if h % STEP_FIELDS == 0:
                    dve.wait_ge(step_kept, 2 + h // STEP_FIELDS + 1)
                make_one_hot(h)
            for h in range(HOT_BUFFERS, len(ONE_HOT)):
                split(h)
            dve.wait_ge(step_kept, 2 + INDEX_STEPS)
            def chunk(c, first, last):
                if not last:
                    tile = c * TILES + TILES
                    if not first:
                        tile = dve.snap(tile)
                    ready_hot_ids(bass.ds(tile, TILES))

                def next_index(t):
                    if not last:
                        dve.wait_ge(batch_ready, c * CHUNK_BATCHES + (t + 1) * BATCHES)
                        ready_index(bass.ds(tile + t, 1), t)

                keep_lookups(c, lambda: next_index(0))
                if first:
                    dve.wait_ge(weights_loaded, 16 * WEIGHTS)
                    nc.vector.tensor_tensor(w1_sb[:, PAIR_TILES, :], w1_sb[:, PAIR_TILES, :], w1_again[:, :],
                                            ALU.add).then_inc(weights_summed, 1)
                if not last:
                    dve.wait_ge(step_kept, c * CHUNK_STEPS + (2 + 2 * INDEX_STEPS))
                    for h in range(HOT_BUFFERS):
                        make_one_hot(h)
                next_index(1)
                if not first:
                    dve.wait_ge(layer_ready, c * LAYER + (2 - LAYER))
                dve.wait_ge(batch_kept, c * CHUNK_BATCHES + (2 + TILES * BATCHES))
                nc.vector.tensor_copy(features[:, PAIR_TILES, :].rearrange("d (q g) -> d q g", q=QUADS),
                                      vectors[:, :, 0].rearrange("d (g q) -> d q g", q=QUADS)).then_inc(dense_kept, 1)

            chunks(dve, chunk)

        @block.scalar
        def _(act):
            act.sem_inc(batch_kept, 2)
            act.sem_inc(step_kept, 2)

            def keep_batch(c, t, b):
                n = t * BATCHES + b
                batch = batch_vectors(b)
                act.wait_ge(batch_ready, c * CHUNK_BATCHES + (n + 1))
                nc.scalar.activation(
                    vectors[:, t * TILE:(t + 1) * TILE, batch[0]:batch[-1] + 1].rearrange("d s v -> d v s"),
                    moved[:, n % 2, 0:len(batch) * TILE].rearrange("d (v s) -> d v s", s=TILE), ACT.Copy)                    .then_inc(batch_kept, 1)

            def keep_indices(step0):
                for s in range(INDEX_STEPS):
                    act.wait_ge(step_ready, step0 + (s + 1))
                    nc.scalar.activation(
                        hot_ids_all[:, s * STEP_FIELDS:(s + 1) * STEP_FIELDS, :].rearrange("p f s -> p (f s)"),
                        gram[:, s % 2, :, :].rearrange("p b x -> p (b x)"), ACT.Copy).then_inc(step_kept, 1)

            def keep_products(c, t, last_chunk, between=lambda s: None):
                for s in range(STEPS):
                    n = tile_step(t, s, last_chunk)
                    first = t * GROUPS + s * STEP_GROUPS
                    act.wait_ge(step_ready, c * CHUNK_STEPS + (n + 1))
                    for q in range(QUADS):
                        part = slice(PAD * q, PAD * (q + 1))
                        same = gram[part, n % 2, :, 0:BANK_GROUPS * QUADS * VECTORS]\
                            .rearrange("p b (g x) -> p b g x", g=BANK_GROUPS)[:, :, :, q * VECTORS:(q + 1) * VECTORS]
                        into = products[part, ::-1, first:first + STEP_GROUPS].rearrange("p j (b g) -> p b g j", b=2)
                        last = nc.scalar.activation(into, same, ACT.Copy)
                    last.then_inc(step_kept, 1)
                    between(s)

            def keep_layers(c, at, between=lambda n: None):
                between(0)
                for half in range(2):
                    act.wait_ge(layer_ready, c * LAYER + (half + 1))
                    for m in range(2 * half, 2 * half + 2):
                        last = nc.scalar.activation(hidden1[:, m, :], mlp[:, half, m % 2, :], ACT.Relu,
                                                    bias=b1_sb[:, m:m + 1])
                    last.then_inc(layer_kept, 1)
                    if half == 0:
                        between(1)
                        between(2)
                between(3)
                for m in range(MTILES2):
                    act.wait_ge(layer_ready, c * LAYER + (3 + m))
                    nc.scalar.activation(hidden2[:, m, :], mlp[:, m, 0, :], ACT.Relu, bias=b2_sb[:, m:m + 1])                        .then_inc(layer_kept, 1)
                between(4)
                act.wait_ge(layer_ready, c * LAYER + 5)
                nc.scalar.activation(
                    y_sb[:, bass.ds(at, CHUNK)].rearrange("o (g q) -> o q g", q=QUADS),
                    mlp[0:1, 0, 1, :].rearrange("o (q g) -> o q g", q=QUADS), ACT.Copy).then_inc(layer_kept, 1)

            def chunk(c, first, last):
                if not first:
                    act.wait_ge(dense_kept, c)
                for b in range(BATCHES):
                    keep_batch(c, 0, b)
                if not last:
                    keep_indices(c * CHUNK_STEPS + INDEX_STEPS)
                if not (first or last):
                    keep_layers(c - 1, c * CHUNK - CHUNK, lambda n: [keep_batch(c, 1, b) for b in IN_LAYERS[n]])
                if not first:
                    act.wait_ge(scratch_written, c * (16 * SCRATCH_DMAS))
                keep_products(c, 0, last, lambda s: [keep_batch(c, 1, b) for b in IN_PRODUCTS[s] if last])
                if first:
                    for b in range(BATCHES):
                        keep_batch(c, 1, b)
                keep_products(c, 1, last)
                if last:
                    keep_layers(c - 1, c * CHUNK - CHUNK)

            keep_indices(0)
            for h in range(len(ONE_HOT)):
                act.wait_ge(table_loaded[h % STAGES], 16 * (h // STAGES + 1))
                nc.scalar.activation(high[:, h, :, :], stage[h % STAGES][0:PART_ROWS, :, :], ACT.Copy)                    .then_inc(high_made, 1)
            act.wait_ge(weights_loaded, 16 * WEIGHTS)
            chunks(act, chunk)
            keep_layers(CHUNKS - 1, (CHUNKS - 1) * CHUNK)


def _w1_order():
    at = {}
    for a in range(VECTORS):
        for b in range(a + 1, VECTORS):
            at[a, b] = DIM + len(at)
    reference = [0] + [f + 1 for f in GATHERED + ONE_HOT]
    order = []
    for delta in range(DELTAS, 0, -1):
        for i in range(VECTORS):
            a, b = reference[i], reference[(i + delta) % VECTORS]
            order.append(at[min(a, b), max(a, b)])
    return order + list(range(DIM)) + list(range(DIM + PAIRS, DIM + PAIRS + DIM))


def kernel(**inputs):
    import numpy as _np
    import concourse.bacc as _bacc
    from concourse import mybir as _mybir
    from concourse.bass_utils import run_bass_kernel_spmd as _run

    nc = _bacc.Bacc("TRN2", target_bir_lowering=False, num_devices=1)
    arrays = {}

    def declare(name, a):
        arrays[f"in_{name}_dram"] = _np.ascontiguousarray(a)
        return nc.dram_tensor(f"in_{name}_dram", a.shape, _mybir.dt.from_np(a.dtype), kind="ExternalInput").ap()

    dense = declare("dense", inputs["r_dense_features"])
    ids = declare("ids", inputs["ids"])
    tables = [declare(f"tbl_{f}", inputs[f"tbl_{f}"]) for f in range(FIELDS)]
    w1 = declare("w1", _np.asarray(inputs["W_top1"])[_w1_order()])

    def columns(name):
        return declare(name, _np.asarray(inputs[name]).reshape(-1, 128).T)

    rest = [columns("b_top1"), declare("W_top2", inputs["W_top2"]), columns("b_top2"), columns("W_top3")]
    out = nc.dram_tensor("out_0_dram", (BATCH, 1), _mybir.dt.float32, kind="ExternalOutput").ap()
    build(nc, dense, ids, tables, w1, *rest, out)
    r = _run(nc, [arrays], core_ids=[0])
    return r.results[0]["out_0_dram"]
```

```python
from contextlib import ExitStack

import concourse.bass as bass
from concourse import mybir

BATCH, DIM = 2048, 128
ROWS = (1250, 125000, 12500, 1250, 1000, 1250, 1250, 12500, 1250, 1000, 1250, 1000, 1000, 12500, 1000, 1250,
        1250, 12500, 12500, 1250, 1000, 1000, 1250, 12500, 12500, 1000)
FIELDS = len(ROWS)
SHORT = 1000
GATHERED = [f for f in range(FIELDS) if ROWS[f] != SHORT]
ONE_HOT = [f for f in range(FIELDS) if ROWS[f] == SHORT]
PARTS = 8
PART_ROWS = SHORT // PARTS
VECTORS = FIELDS + 1
TRANSPOSED = 1 + len(GATHERED)
PAIRS = VECTORS * (VECTORS - 1) // 2
DELTAS = VECTORS // 2
TILE = 128
TILES = 2
CHUNK = TILES * TILE
CHUNKS = BATCH // CHUNK
QUADS = 4
PRODUCT = QUADS * VECTORS
GROUPS = TILE // QUADS
CHUNK_GROUPS = CHUNK // QUADS
BANK = 512
BATCH_VECTORS = BANK // TILE
BATCHES = -(-TRANSPOSED // BATCH_VECTORS)
HOT_FIELDS = BANK // CHUNK
HOT_BATCHES = -(-len(ONE_HOT) // HOT_FIELDS)
LAYER = 5
HOT_BUFFERS = 4
BANK_GROUPS = 4
STEP_GROUPS = 2 * BANK_GROUPS
STEPS = GROUPS // STEP_GROUPS
STEP_FIELDS = 2 * BANK // CHUNK
INDEX_STEPS = len(ONE_HOT) // STEP_FIELDS
HIDDEN1, HIDDEN2 = 512, 256
PAIR_TILES = 3
PAIR_ROWS = PAIRS // PAIR_TILES
KTILES = PAIR_TILES + 1
MTILES1, MTILES2 = HIDDEN1 // 128, HIDDEN2 // 128
TILE0_AFTER = (1, 3, 4, 5, 6)
IN_LAYERS = ((0,), (1,), (2,), (3,), (4,))
IN_PRODUCTS = ((0,), (1, 2), (3, 4), ())
IN_FIRST_PRODUCTS = ((0,), (1,), (2,), (3, 4))

WRAP = VECTORS + DELTAS - 1
SLOT = QUADS * CHUNK_GROUPS
SLOTS = VECTORS * WRAP + (VECTORS + 1) * (VECTORS - 1) + 1
FIRST_SLOT = VECTORS * (WRAP - DELTAS)


def batch_vectors(b):
    return range(b * BATCH_VECTORS, min((b + 1) * BATCH_VECTORS, TRANSPOSED))


def build(nc, dense, ids, tables, w1, b1, w2, b2, w3, out):
    fp32, fp32r, fp16, int32 = mybir.dt.float32, mybir.dt.float32r, mybir.dt.float16, mybir.dt.int32
    ALU, ACT = mybir.AluOpType, mybir.ActivationFunctionType

    scratch = nc.dram_tensor("scratch", (SLOTS, QUADS, CHUNK_GROUPS), fp32, kind="Internal").ap()

    with ExitStack() as ctx:
        def sb(name, shape, dt=fp32):
            return ctx.enter_context(nc.sbuf_tensor(name, shape, dt))

        def ps(name, shape):
            return ctx.enter_context(nc.psum_tensor(name, shape, fp32))

        def sem(name):
            return ctx.enter_context(nc.semaphore(name))

        identity = sb("identity", [128, 128])
        identity16 = sb("identity16", [128, 128], fp16)
        ones = sb("ones", [128, 1])
        row_of_int = sb("row_of_int", [128, PARTS], int32)
        row_of = sb("row_of", [128, PARTS])
        ids_sb = sb("ids_sb", [TILE, BATCH // TILE, FIELDS], int32)
        index = [sb(f"index{t}", [TILE, FIELDS], int32) for t in range(TILES)]
        hot_ids = sb("hot_ids", [TILE, TILES, len(ONE_HOT)], fp16)
        hot_ids_all = sb("hot_ids_all", [128, len(ONE_HOT), CHUNK])
        one_hot = sb("one_hot", [PART_ROWS, HOT_BUFFERS, PARTS, CHUNK], fp32r)
        high = sb("high", [PART_ROWS, len(ONE_HOT), PARTS, DIM], fp32r)
        low = sb("low", [PART_ROWS, len(ONE_HOT), PARTS, DIM], fp32r)
        rows = [sb(f"rows{t}", [TILE, TRANSPOSED, DIM]) for t in range(TILES)]
        vectors = sb("vectors", [DIM, CHUNK, VECTORS])
        products = sb("products", [128, PRODUCT, CHUNK_GROUPS])
        features = sb("features", [128, KTILES, CHUNK])
        w1_sb = sb("w1_sb", [128, KTILES, HIDDEN1])
        w2_sb = sb("w2_sb", [128, MTILES1, HIDDEN2])
        w3_sb = sb("w3_sb", [128, MTILES2])
        b1_sb = sb("b1_sb", [128, MTILES1])
        b2_sb = sb("b2_sb", [128, MTILES2])
        hidden1 = sb("hidden1", [128, MTILES1, CHUNK])
        hidden2 = sb("hidden2", [128, MTILES2, CHUNK])
        weighted = sb("weighted", [128, CHUNK])
        y_sb = sb("y_sb", [1, CHUNK])
        part_columns = DIM // CHUNK_GROUPS
        stage = [products[:, h * PARTS * part_columns:(h + 1) * PARTS * part_columns, :]
                 .rearrange("p (k a) g -> p k (a g)", k=PARTS) for h in range(PRODUCT // (PARTS * part_columns))]
        stage += [x[:, :, :].rearrange("p k (h d) -> p (k h) d", d=DIM) for x in (features, hidden1)]
        assert len(stage) == len(ONE_HOT)
        w1_again = hidden2[:, :, :].rearrange("p m n -> p (m n)")

        moved = ps("moved", [128, 2, BANK])
        gram = ps("gram", [128, 2, 2, BANK])
        mlp = ps("mlp", [128, 2, 2, CHUNK])

        ids_loaded = sem("ids_loaded")
        dense_loaded = [sem(f"dense_loaded{t}") for t in range(TILES)]
        table_loaded = [sem(f"table_loaded{n}") for n in range(len(ONE_HOT))]
        weights_loaded = sem("weights_loaded")
        constants_made = sem("constants_made")
        identity16_made = sem("identity16_made")
        index_ready = [sem(f"index_ready{t}") for t in range(TILES)]
        hot_ids_ready = sem("hot_ids_ready")
        rows_loaded = [[sem(f"rows_loaded{t}_{b}") for b in range(BATCHES)] for t in range(TILES)]
        high_made = sem("high_made")
        low_made = sem("low_made")
        rows_numbered = sem("rows_numbered")
        weights_summed = sem("weights_summed")
        dense_kept = sem("dense_kept")
        one_hot_made = sem("one_hot_made")
        batch_ready = sem("batch_ready")
        batch_kept = sem("batch_kept")
        hot_ready = sem("hot_ready")
        hot_kept = sem("hot_kept")
        step_ready = sem("step_ready")
        step_kept = sem("step_kept")
        scratch_written = sem("scratch_written")
        pairs_loaded = sem("pairs_loaded")
        layer_ready = sem("layer_ready")
        layer_kept = sem("layer_kept")
        half_weighted = sem("half_weighted")
        weighted_made = sem("weighted_made")
        out_written = sem("out_written")

        CHUNK_BATCHES = TILES * BATCHES
        CHUNK_STEPS = TILES * STEPS + INDEX_STEPS
        assert CHUNK_BATCHES % 2 == CHUNK_STEPS % 2 == HOT_BATCHES % 2 == INDEX_STEPS % 2 == 0
        SCRATCH_DMAS = 2 * QUADS
        WEIGHTS = 7
        CONSTANTS = 4

        def tile_step(t, s, last):
            return (1 if last else 2) * INDEX_STEPS + t * STEPS + s

        def chunks(engine, chunk):
            chunk(0, True, False)
            with engine.Fori(1, CHUNKS - 1) as c:
                chunk(c, False, False)
            chunk(CHUNKS - 1, False, True)

        block = ctx.enter_context(nc.Block())

        @block.sync
        def _(sp):
            def load_dense(at, t):
                sp.dma_start(rows[t][:, 0, :], dense[bass.ds(at, TILE), :]).then_inc(dense_loaded[t], 16)

            def load_table(n):
                sp.dma_start(stage[n][0:PART_ROWS, :, :],
                             tables[ONE_HOT[n]].rearrange("(p k) d -> p k d", k=PARTS))\
                    .then_inc(table_loaded[n], 16)

            def store_y(at):
                sp.dma_start(out[bass.ds(at, CHUNK), :].rearrange("b o -> o b"), y_sb[:, :]).then_inc(out_written, 16)

            sp.dma_start(ids_sb[:, :, :], ids.rearrange("(t p) f -> p t f", p=TILE)).then_inc(ids_loaded, 16)
            sp.sem_inc(out_written, 16)
            for n in range(len(ONE_HOT)):
                load_table(n)
                if n == 2:
                    for t in range(TILES):
                        load_dense(t * TILE, t)
            for into, source in (
                (w1_sb[0:PAIR_ROWS, 0:PAIR_TILES, :], w1[0:PAIRS, :].rearrange("(k p) n -> p k n", p=PAIR_ROWS)),
                (w1_sb[:, PAIR_TILES, :], w1[PAIRS:PAIRS + DIM, :]),
                (w1_again, w1[PAIRS + DIM:PAIRS + 2 * DIM, :]),
                (w2_sb[:, :, :], w2.rearrange("(k p) n -> p k n", p=128)),
                (w3_sb[:, :], w3),
                (b1_sb[:, :], b1),
                (b2_sb[:, :], b2),
            ):
                sp.dma_start(into, source).then_inc(weights_loaded, 16)

            def chunk(c, first, last):
                if not first:
                    sp.wait_ge(pairs_loaded, c * 16)
                if not last:
                    for t in range(TILES):
                        at = c * CHUNK + (CHUNK + t * TILE)
                        if not first:
                            at = sp.snap(at)
                        sp.wait_ge(batch_ready, c * CHUNK_BATCHES + (t * BATCHES + 1))
                        load_dense(at, t)
                if not (first or last):
                    sp.wait_ge(layer_kept, c * LAYER)
                    store_y(sp.snap(c * CHUNK - CHUNK))
                sp.wait_ge(step_kept, c * CHUNK_STEPS + (2 + tile_step(1, STEPS, last)))
                for q in range(QUADS):
                    part = slice(VECTORS * q, VECTORS * (q + 1))
                    block_column = VECTORS * (QUADS - 1 - q)
                    for first_column, slot in ((0, VECTORS * (WRAP - VECTORS + 1)), (VECTORS - DELTAS, 0)):
                        into = bass.AP(scratch.tensor, slot * SLOT + q * CHUNK_GROUPS,
                                       [[(VECTORS + 1) * SLOT, VECTORS], [VECTORS * SLOT, VECTORS - first_column],
                                        [1, CHUNK_GROUPS]])
                        sp.dma_start(into, products[part, block_column + first_column:block_column + VECTORS, :])\
                            .then_inc(scratch_written, 16)
                if not first:
                    sp.wait_ge(layer_ready, c * LAYER + (2 - LAYER))
                sp.wait_ge(scratch_written, c * (16 * SCRATCH_DMAS) + 16 * SCRATCH_DMAS)
                sp.dma_start(features[0:PAIR_ROWS, 0:PAIR_TILES, :],
                             scratch[FIRST_SLOT:FIRST_SLOT + PAIRS, :, :]
                             .rearrange("(k p) q g -> p k (q g)", p=PAIR_ROWS)).then_inc(pairs_loaded, 16)

            chunks(sp, chunk)
            for c in (CHUNKS - 2, CHUNKS - 1):
                sp.wait_ge(layer_kept, LAYER * (c + 1))
                store_y(c * CHUNK)
            sp.wait_ge(out_written, 16 * (CHUNKS + 1))

        @block.gpsimd
        def _(pool):
            nc.gpsimd.memset(identity[:, :], 0.0).then_inc(constants_made, 1)
            nc.gpsimd.iota(row_of_int[:, :], pattern=[[1, PARTS]], base=0, channel_multiplier=PARTS)\
                .then_inc(constants_made, 1)
            nc.gpsimd.memset(ones[:, :], 1.0).then_inc(constants_made, 1)
            pool.wait_ge(constants_made, CONSTANTS - 1)
            nc.gpsimd.affine_select(out=identity[:, :], in_=identity[:, :], compare_op=ALU.not_equal, fill=1.0,
                                    base=0, pattern=[[-1, 128]], channel_multiplier=1).then_inc(constants_made, 1)

            def gather(t, b):
                for v in batch_vectors(b):
                    if v:
                        f = GATHERED[v - 1]
                        pool.indirect_dma_start(
                            rows[t][:, v, :], None, tables[f][:, :],
                            bass.IndirectOffsetOnAxis(ap=index[t][:, f:f + 1], axis=0),
                        ).then_inc(rows_loaded[t][b], 16)

            for t in range(TILES):
                pool.wait_ge(index_ready[t], 1)
                for b in range(BATCHES):
                    gather(t, b)
            batches = pool.alloc_register("batches")
            pool.reg_mov(batches, 1)
            with pool.Fori(1, CHUNKS) as c:
                for t in range(TILES):
                    for b in range(BATCHES):
                        count = pool.snap(batches)
                        if b == 0:
                            pool.wait_ge(index_ready[t], c + 1)
                        pool.wait_ge(batch_ready, count)
                        pool.reg_add(batches, batches, 1)
                        gather(t, b)

        @block.tensor
        def _(pe):
            def transpose_batch(c, t, b):
                n = t * BATCHES + b
                batch = batch_vectors(b)
                gathers = len(batch) - (b == 0)
                pe.wait_ge(rows_loaded[t][b], c * (16 * gathers) + 16 * gathers)
                if b == 0:
                    pe.wait_ge(dense_loaded[t], c * 16 + 16)
                pe.wait_ge(batch_kept, c * CHUNK_BATCHES + (n + 1))
                for m, v in enumerate(batch):
                    last = nc.tensor.transpose(moved[:, n % 2, m * TILE:(m + 1) * TILE], rows[t][:, v, :],
                                               identity[:, :])
                last.then_inc(batch_ready, 1)

            def multiply(c, t, last_chunk, between=lambda s: None):
                pe.wait_ge(batch_kept, c * CHUNK_BATCHES + (2 + (t + 1) * BATCHES))
                if t == 0:
                    pe.wait_ge(hot_kept, c * HOT_BATCHES + (2 + HOT_BATCHES))
                for s in range(STEPS):
                    n = tile_step(t, s, last_chunk)
                    pe.wait_ge(step_kept, c * CHUNK_STEPS + (n + 1))
                    for g in range(STEP_GROUPS):
                        at = t * TILE + (s * STEP_GROUPS + g) * QUADS
                        bank, col = divmod(g, BANK_GROUPS)
                        four = vectors[:, at:at + QUADS, :].rearrange("d s v -> d (s v)")
                        last = nc.tensor.matmul(gram[0:PRODUCT, n % 2, bank, col * PRODUCT:(col + 1) * PRODUCT],
                                                four, four, start=True, stop=True)
                    last.then_inc(step_ready, 1)
                    between(s)

            def broadcast_indices(c, step0):
                pe.wait_ge(hot_ids_ready, c + 1)
                for s in range(INDEX_STEPS):
                    n = step0 + s
                    pe.wait_ge(step_kept, n + 1)
                    for m in range(STEP_FIELDS):
                        h = s * STEP_FIELDS + m
                        bank, col = divmod(m * CHUNK, BANK)
                        for t in range(TILES):
                            last = nc.tensor.matmul(gram[:, s % 2, bank, col + t * TILE:col + (t + 1) * TILE],
                                                    hot_ids[:, t, h:h + 1].broadcast_to([TILE, 128]),
                                                    identity16[:, :], start=True, stop=True)
                    last.then_inc(step_ready, 1)

            def look_up(c, h, first_chunk):
                j, m = divmod(h, HOT_FIELDS)
                if first_chunk:
                    pe.wait_ge(high_made, h + 1)
                if m == 0:
                    pe.wait_ge(hot_kept, c * HOT_BATCHES + (j + 1))
                pe.wait_ge(one_hot_made, c * len(ONE_HOT) + (h + 1))
                for part in (high, low):
                    if first_chunk and part is low:
                        pe.wait_ge(low_made, h + 1)
                    for k in range(PARTS):
                        last = nc.tensor.matmul(mlp[:, j % 2, m, :], part[:, h, k, :],
                                                one_hot[:, h % HOT_BUFFERS, k, :],
                                                start=(part is high and k == 0),
                                                stop=(part is low and k == PARTS - 1))
                if m == HOT_FIELDS - 1:
                    last.then_inc(hot_ready, 1)

            def layers(c, between, lookups):
                pe.wait_ge(pairs_loaded, c * 16 + 16)
                pe.wait_ge(dense_kept, c + 1)
                if lookups is None:
                    pe.wait_ge(layer_kept, c * LAYER)
                for m in range(MTILES1):
                    if m % 2 == 0 and lookups is not None:
                        pe.wait_ge(hot_kept, lookups * HOT_BATCHES + (2 + HOT_BATCHES - 1 + m // 2))
                    for k in range(KTILES):
                        height = PAIR_ROWS if k < PAIR_TILES else DIM
                        last = nc.tensor.matmul(mlp[:, m // 2, m % 2, :],
                                                w1_sb[0:height, k, m * 128:(m + 1) * 128],
                                                features[0:height, k, :], start=(k == 0), stop=(k == KTILES - 1))
                    if m % 2:
                        last.then_inc(layer_ready, 1)
                    between(m)
                for m in range(MTILES2):
                    for k in range(MTILES1):
                        if m == 0 and k % 2 == 0:
                            pe.wait_ge(layer_kept, c * LAYER + (1 + k // 2))
                        last = nc.tensor.matmul(mlp[:, m, 0, :], w2_sb[:, k, m * 128:(m + 1) * 128],
                                                hidden1[:, k, :], start=(k == 0), stop=(k == MTILES1 - 1))
                    last.then_inc(layer_ready, 1)
                between(4)

            def last_layer(c):
                pe.wait_ge(weighted_made, c + 1)
                nc.tensor.matmul(mlp[0:1, 1, 1, :], ones[:, :], weighted[:, :], start=True, stop=True)\
                    .then_inc(layer_ready, 1)

            def chunk(c, first, last):
                for h in range(len(ONE_HOT)):
                    look_up(c, h, first)
                    if h in TILE0_AFTER:
                        transpose_batch(c, 0, TILE0_AFTER.index(h))
                if not last:
                    broadcast_indices(c + 1, c * CHUNK_STEPS + INDEX_STEPS)
                if first:
                    pe.wait_ge(weights_summed, 1)
                    multiply(c, 0, last, lambda s: [transpose_batch(c, 1, b) for b in IN_FIRST_PRODUCTS[s]])
                elif not last:
                    layers(c - 1, lambda n: [transpose_batch(c, 1, b) for b in IN_LAYERS[n]], c)
                    multiply(c, 0, last)
                    last_layer(c - 1)
                else:
                    multiply(c, 0, last, lambda s: [transpose_batch(c, 1, b) for b in IN_PRODUCTS[s]])
                multiply(c, 1, last)
                if last:
                    layers(c - 1, lambda n: None, None)
                    last_layer(c - 1)

            pe.wait_ge(identity16_made, 1)
            broadcast_indices(0, 0)
            chunks(pe, chunk)
            layers(CHUNKS - 1, lambda n: None, None)
            last_layer(CHUNKS - 1)

        @block.vector
        def _(dve):
            def ready_index(tile, t):
                nc.vector.tensor_copy(index[t][:, :], ids_sb[:, tile, :]).then_inc(index_ready[t], 1)

            def ready_hot_ids(tiles):
                runs = []
                for h, f in enumerate(ONE_HOT):
                    if runs and ONE_HOT[runs[-1][0]] + runs[-1][1] == f:
                        runs[-1][1] += 1
                    else:
                        runs.append([h, 1])
                for h, count in runs:
                    last = nc.vector.tensor_copy(hot_ids[:, :, h:h + count],
                                                 ids_sb[:, tiles, ONE_HOT[h]:ONE_HOT[h] + count])
                last.then_inc(hot_ids_ready, 1)

            def make_one_hot(h):
                for k in range(PARTS):
                    last = nc.vector.tensor_scalar(one_hot[:, h % HOT_BUFFERS, k, :], hot_ids_all[0:PART_ROWS, h, :],
                                                   row_of[0:PART_ROWS, k:k + 1], None, ALU.is_equal)
                last.then_inc(one_hot_made, 1)

            def keep_lookups(c, first, and_then):
                made = HOT_BUFFERS
                for j in range(HOT_BATCHES):
                    if j == HOT_BATCHES - 1:
                        and_then()
                    dve.wait_ge(hot_ready, c * HOT_BATCHES + (j + 1))
                    v = TRANSPOSED + j * HOT_FIELDS
                    nc.vector.tensor_copy(vectors[:, :, v:v + HOT_FIELDS].rearrange("d s v -> d v s"),
                                          mlp[:, j % 2, :, :]).then_inc(hot_kept, 1)
                    for _ in range(HOT_FIELDS):
                        if made < len(ONE_HOT):
                            make_one_hot(made)
                            if first:
                                split(made)
                            made += 1

            def split(h):
                dve.wait_ge(high_made, h + 1)
                nc.vector.tensor_tensor(low[:, h, :, :], stage[h][0:PART_ROWS, :, :],
                                        high[:, h, :, :].bitcast(fp32), ALU.subtract).then_inc(low_made, 1)

            def weigh(c):
                dve.wait_ge(layer_kept, c * LAYER + 3)
                nc.vector.tensor_scalar(weighted[:, :], hidden2[:, 0, :], w3_sb[:, 0:1], None, ALU.mult)\
                    .then_inc(half_weighted, 1)
                dve.wait_ge(half_weighted, c + 1)
                dve.wait_ge(layer_kept, c * LAYER + 4)
                nc.vector.scalar_tensor_tensor(weighted[:, :], hidden2[:, 1, :], w3_sb[:, 1:2], weighted[:, :],
                                               ALU.mult, ALU.add).then_inc(weighted_made, 1)

            dve.sem_inc(hot_kept, 2)
            dve.wait_ge(ids_loaded, 16)
            for t in range(TILES):
                ready_index(t, t)
            ready_hot_ids(slice(0, TILES))
            dve.wait_ge(constants_made, CONSTANTS)
            nc.vector.tensor_copy(row_of[:, :], row_of_int[:, :]).then_inc(rows_numbered, 1)
            nc.vector.tensor_copy(identity16[:, :], identity[:, :]).then_inc(identity16_made, 1)
            dve.wait_ge(step_ready, 1)
            dve.wait_ge(step_kept, 2)
            nc.vector.tensor_copy(hot_ids_all[:, 0:STEP_FIELDS, :].rearrange("p f s -> p (f s)"),
                                  gram[:, 0, :, :].rearrange("p b x -> p (b x)")).then_inc(step_kept, 1)
            dve.wait_ge(rows_numbered, 1)
            dve.wait_ge(step_kept, 3)
            assert HOT_BUFFERS == STEP_FIELDS
            for h in range(HOT_BUFFERS):
                make_one_hot(h)
                split(h)
            dve.wait_ge(step_kept, 2 + INDEX_STEPS)

            def chunk(c, first, last):
                tile = c * TILES + TILES
                if not first:
                    tile = dve.snap(tile)

                def next_indices():
                    if not last:
                        ready_hot_ids(bass.ds(tile, TILES))
                    next_index(0)

                def next_index(t):
                    if not last:
                        dve.wait_ge(batch_ready, c * CHUNK_BATCHES + (t + 1) * BATCHES)
                        ready_index(bass.ds(tile + t, 1), t)

                keep_lookups(c, first, next_indices)
                if first:
                    dve.wait_ge(weights_loaded, 16 * WEIGHTS)
                    nc.vector.tensor_tensor(w1_sb[:, PAIR_TILES, :], w1_sb[:, PAIR_TILES, :], w1_again[:, :],
                                            ALU.add).then_inc(weights_summed, 1)
                if not last:
                    dve.wait_ge(step_kept, c * CHUNK_STEPS + (2 + 2 * INDEX_STEPS))
                    for h in range(HOT_BUFFERS):
                        make_one_hot(h)
                next_index(1)
                if not (first or last):
                    weigh(c - 1)
                if not first:
                    dve.wait_ge(layer_ready, c * LAYER + (2 - LAYER))
                dve.wait_ge(batch_kept, c * CHUNK_BATCHES + (2 + TILES * BATCHES))
                nc.vector.tensor_copy(features[:, PAIR_TILES, :].rearrange("d (q g) -> d q g", q=QUADS),
                                      vectors[:, :, 0].rearrange("d (g q) -> d q g", q=QUADS)).then_inc(dense_kept, 1)

            chunks(dve, chunk)
            for c in (CHUNKS - 2, CHUNKS - 1):
                weigh(c)

        @block.scalar
        def _(act):
            act.sem_inc(batch_kept, 2)
            act.sem_inc(step_kept, 2)

            def keep_batch(c, t, b):
                n = t * BATCHES + b
                batch = batch_vectors(b)
                act.wait_ge(batch_ready, c * CHUNK_BATCHES + (n + 1))
                nc.scalar.activation(
                    vectors[:, t * TILE:(t + 1) * TILE, batch[0]:batch[-1] + 1].rearrange("d s v -> d v s"),
                    moved[:, n % 2, 0:len(batch) * TILE].rearrange("d (v s) -> d v s", s=TILE), ACT.Copy)\
                    .then_inc(batch_kept, 1)

            def keep_indices(step0, first=0):
                for s in range(first, INDEX_STEPS):
                    act.wait_ge(step_ready, step0 + (s + 1))
                    nc.scalar.activation(
                        hot_ids_all[:, s * STEP_FIELDS:(s + 1) * STEP_FIELDS, :].rearrange("p f s -> p (f s)"),
                        gram[:, s % 2, :, :].rearrange("p b x -> p (b x)"), ACT.Copy).then_inc(step_kept, 1)

            def keep_products(c, t, last_chunk, between=lambda s: None):
                for s in range(STEPS):
                    n = tile_step(t, s, last_chunk)
                    first = t * GROUPS + s * STEP_GROUPS
                    act.wait_ge(step_ready, c * CHUNK_STEPS + (n + 1))
                    nc.scalar.activation(
                        products[0:PRODUCT, ::-1, first:first + STEP_GROUPS].rearrange("p x (b g) -> p b g x", b=2),
                        gram[0:PRODUCT, n % 2, :, 0:BANK_GROUPS * PRODUCT]
                        .rearrange("p b (g x) -> p b g x", g=BANK_GROUPS), ACT.Copy).then_inc(step_kept, 1)
                    between(s)

            def keep_layers(c, between=lambda n: None):
                between(0)
                for half in range(2):
                    act.wait_ge(layer_ready, c * LAYER + (half + 1))
                    for m in range(2 * half, 2 * half + 2):
                        last = nc.scalar.activation(hidden1[:, m, :], mlp[:, half, m % 2, :], ACT.Relu,
                                                    bias=b1_sb[:, m:m + 1])
                    last.then_inc(layer_kept, 1)
                    if half == 0:
                        between(1)
                        between(2)
                between(3)
                for m in range(MTILES2):
                    act.wait_ge(layer_ready, c * LAYER + (3 + m))
                    nc.scalar.activation(hidden2[:, m, :], mlp[:, m, 0, :], ACT.Relu, bias=b2_sb[:, m:m + 1])\
                        .then_inc(layer_kept, 1)
                between(4)

            def keep_y(c):
                act.wait_ge(layer_ready, c * LAYER + 5)
                act.wait_ge(out_written, c * 16 + 16)
                nc.scalar.activation(
                    y_sb[:, :].rearrange("o (g q) -> o q g", q=QUADS),
                    mlp[0:1, 1, 1, :].rearrange("o (q g) -> o q g", q=QUADS), ACT.Copy).then_inc(layer_kept, 1)

            def chunk(c, first, last):
                if not first:
                    act.wait_ge(dense_kept, c)
                for b in range(BATCHES):
                    keep_batch(c, 0, b)
                if not last:
                    keep_indices(c * CHUNK_STEPS + INDEX_STEPS)
                if not (first or last):
                    keep_layers(c - 1, lambda n: [keep_batch(c, 1, b) for b in IN_LAYERS[n]])
                if not first:
                    act.wait_ge(scratch_written, c * (16 * SCRATCH_DMAS))
                batches = IN_FIRST_PRODUCTS if first else IN_PRODUCTS if last else STEPS * ((),)
                keep_products(c, 0, last, lambda s: [keep_batch(c, 1, b) for b in batches[s]])
                if not (first or last):
                    keep_y(c - 1)
                keep_products(c, 1, last)
                if last:
                    keep_layers(c - 1)
                    keep_y(c - 1)

            for h in range(len(ONE_HOT)):
                act.wait_ge(table_loaded[h], 16)
                nc.scalar.activation(high[:, h, :, :], stage[h][0:PART_ROWS, :, :], ACT.Copy).then_inc(high_made, 1)
                if h == 1:
                    act.wait_ge(step_kept, 3)
                    keep_indices(0, 1)
            act.wait_ge(weights_loaded, 16 * WEIGHTS)
            chunks(act, chunk)
            keep_layers(CHUNKS - 1)
            keep_y(CHUNKS - 1)


def _w1_order():
    at = {}
    for a in range(VECTORS):
        for b in range(a + 1, VECTORS):
            at[a, b] = DIM + len(at)
    reference = [0] + [f + 1 for f in GATHERED + ONE_HOT]
    order = []
    for delta in range(DELTAS, 0, -1):
        for i in range(VECTORS):
            a, b = reference[i], reference[(i + delta) % VECTORS]
            order.append(at[min(a, b), max(a, b)])
    return order + list(range(DIM)) + list(range(DIM + PAIRS, DIM + PAIRS + DIM))


def kernel(**inputs):
    import numpy as _np
    import concourse.bacc as _bacc
    from concourse import mybir as _mybir
    from concourse.bass_utils import run_bass_kernel_spmd as _run

    nc = _bacc.Bacc("TRN2", target_bir_lowering=False, num_devices=1)
    arrays = {}

    def declare(name, a):
        arrays[f"in_{name}_dram"] = _np.ascontiguousarray(a)
        return nc.dram_tensor(f"in_{name}_dram", a.shape, _mybir.dt.from_np(a.dtype), kind="ExternalInput").ap()

    dense = declare("dense", inputs["r_dense_features"])
    ids = declare("ids", inputs["ids"])
    tables = [declare(f"tbl_{f}", inputs[f"tbl_{f}"]) for f in range(FIELDS)]
    w1 = declare("w1", _np.asarray(inputs["W_top1"])[_w1_order()])

    def columns(name):
        return declare(name, _np.asarray(inputs[name]).reshape(-1, 128).T)

    rest = [columns("b_top1"), declare("W_top2", inputs["W_top2"]), columns("b_top2"), columns("W_top3")]
    out = nc.dram_tensor("out_0_dram", (BATCH, 1), _mybir.dt.float32, kind="ExternalOutput").ap()
    build(nc, dense, ids, tables, w1, *rest, out)
    r = _run(nc, [arrays], core_ids=[0])
    return r.results[0]["out_0_dram"]
```

```python
from contextlib import ExitStack

import concourse.bass as bass
from concourse import mybir

BATCH, DIM = 2048, 128
ROWS = (1250, 125000, 12500, 1250, 1000, 1250, 1250, 12500, 1250, 1000, 1250, 1000, 1000, 12500, 1000, 1250,
        1250, 12500, 12500, 1250, 1000, 1000, 1250, 12500, 12500, 1000)
FIELDS = len(ROWS)
SHORT = 1000
GATHERED = [f for f in range(FIELDS) if ROWS[f] != SHORT]
ONE_HOT = [f for f in range(FIELDS) if ROWS[f] == SHORT]
PARTS = 8
PART_ROWS = SHORT // PARTS
VECTORS = FIELDS + 1
TRANSPOSED = len(GATHERED)
DENSE = VECTORS - 1
PAIRS = VECTORS * (VECTORS - 1) // 2
DELTAS = VECTORS // 2
TILE = 128
TILES = 2
CHUNK = TILES * TILE
CHUNKS = BATCH // CHUNK
QUADS = 4
PRODUCT = QUADS * VECTORS
GROUPS = TILE // QUADS
CHUNK_GROUPS = CHUNK // QUADS
BANK = 512
BATCH_VECTORS = BANK // TILE
BATCHES = -(-TRANSPOSED // BATCH_VECTORS)
HOT_FIELDS = BANK // CHUNK
HOT_BATCHES = len(ONE_HOT) // HOT_FIELDS
LAYER = 5
HOT_BUFFERS = 4
BANK_GROUPS = 4
STEP_GROUPS = 2 * BANK_GROUPS
STEPS = GROUPS // STEP_GROUPS
SWING = ONE_HOT[0]
HIDDEN1, HIDDEN2 = 512, 256
PAIR_TILES = 3
PAIR_ROWS = PAIRS // PAIR_TILES
KTILES = PAIR_TILES + 1
MTILES1, MTILES2 = HIDDEN1 // 128, HIDDEN2 // 128
EARLY = HOT_FIELDS
TILE0_AFTER = (2, 3, 4, 5, 6)
TILE0_AFTER_FIRST = (3, 4, 5, 6, 7)
IN_LAYERS = ((), (), (), (0,), (1,))
IN_PRODUCTS = ((), (2,), (3,), (4,), ())
IN_LAST_PRODUCTS = ((0,), (1,), (2,), (3, 4), ())
IN_FIRST_PRODUCTS = ((0,), (1,), (), (), (2,))
LATE_FIRST = (3, 4)

WRAP = VECTORS + DELTAS - 1
SLOT = QUADS * CHUNK_GROUPS
SLOTS = VECTORS * WRAP + (VECTORS + 1) * (VECTORS - 1) + 1
FIRST_SLOT = VECTORS * (WRAP - DELTAS)


def batch_vectors(b, swing):
    return range(b * BATCH_VECTORS, min((b + 1) * BATCH_VECTORS, TRANSPOSED + swing))


def build(nc, dense, ids, ids_of_field, tables, w1, b1, w2, b2, w3, out):
    fp32, fp32r, int32 = mybir.dt.float32, mybir.dt.float32r, mybir.dt.int32
    ALU, ACT = mybir.AluOpType, mybir.ActivationFunctionType

    scratch = nc.dram_tensor("scratch", (SLOTS, QUADS, CHUNK_GROUPS), fp32, kind="Internal").ap()

    with ExitStack() as ctx:
        def sb(name, shape, dt=fp32):
            return ctx.enter_context(nc.sbuf_tensor(name, shape, dt))

        def ps(name, shape):
            return ctx.enter_context(nc.psum_tensor(name, shape, fp32))

        def sem(name):
            return ctx.enter_context(nc.semaphore(name))

        identity = sb("identity", [128, 128])
        ones = sb("ones", [128, 1])
        row_of_int = sb("row_of_int", [128, 1], int32)
        row_of = sb("row_of", [128, 1])
        ids_sb = sb("ids_sb", [TILE, BATCH // TILE, FIELDS], int32)
        index = [sb(f"index{t}", [TILE, FIELDS], int32) for t in range(TILES)]
        hot_ids = sb("hot_ids", [128, len(ONE_HOT), CHUNK], int32)
        one_hot = sb("one_hot", [PART_ROWS, HOT_BUFFERS, PARTS, CHUNK], fp32r)
        high = sb("high", [PART_ROWS, len(ONE_HOT), PARTS, DIM], fp32r)
        low = sb("low", [PART_ROWS, len(ONE_HOT), PARTS, DIM], fp32r)
        rows = [sb(f"rows{t}", [TILE, TRANSPOSED + 1, DIM]) for t in range(TILES)]
        vectors = sb("vectors", [DIM, CHUNK, VECTORS])
        products = sb("products", [128, PRODUCT, CHUNK_GROUPS])
        dense_sb = sb("dense_sb", [DIM, CHUNK])
        features = sb("features", [128, KTILES, CHUNK])
        w1_sb = sb("w1_sb", [128, KTILES, HIDDEN1])
        w2_sb = sb("w2_sb", [128, MTILES1, HIDDEN2])
        w3_sb = sb("w3_sb", [128, MTILES2])
        b1_sb = sb("b1_sb", [128, MTILES1])
        b2_sb = sb("b2_sb", [128, MTILES2])
        hidden1 = sb("hidden1", [128, MTILES1, CHUNK])
        hidden2 = sb("hidden2", [128, MTILES2, CHUNK])
        weighted = sb("weighted", [128, CHUNK])
        y_sb = sb("y_sb", [1, CHUNK])
        part_columns = DIM // CHUNK_GROUPS
        stage = [products[:, h * PARTS * part_columns:(h + 1) * PARTS * part_columns, :]
                 .rearrange("p (k a) g -> p k (a g)", k=PARTS) for h in range(PRODUCT // (PARTS * part_columns))]
        stage += [x[:, :, :].rearrange("p k (h d) -> p (k h) d", d=DIM) for x in (features, hidden1)]
        assert len(stage) == len(ONE_HOT)
        w1_again = hidden2[:, :, :].rearrange("p m n -> p (m n)")

        moved = ps("moved", [128, 2, BANK])
        gram = ps("gram", [128, 2, 2, BANK])
        mlp = ps("mlp", [128, 2, 2, CHUNK])

        ids_loaded = [sem(f"ids_loaded{n}") for n in range(2)]
        hot_ids_loaded = [sem(f"hot_ids_loaded{n}") for n in range(2)]
        dense_loaded = sem("dense_loaded")
        table_loaded = [sem(f"table_loaded{n}") for n in range(len(ONE_HOT))]
        weights_loaded = sem("weights_loaded")
        constants_made = sem("constants_made")
        index_ready = [sem(f"index_ready{t}") for t in range(TILES)]
        rows_loaded = [[sem(f"rows_loaded{t}_{b}") for b in range(BATCHES)] for t in range(TILES)]
        swing_loaded = [sem(f"swing_loaded{t}") for t in range(TILES)]
        high_made = sem("high_made")
        low_made = sem("low_made")
        rows_numbered = sem("rows_numbered")
        hot_ids_shifted = sem("hot_ids_shifted")
        weights_summed = sem("weights_summed")
        dense_kept = sem("dense_kept")
        one_hot_made = sem("one_hot_made")
        batch_ready = sem("batch_ready")
        batch_kept = sem("batch_kept")
        hot_ready = sem("hot_ready")
        hot_kept = sem("hot_kept")
        step_ready = sem("step_ready")
        step_kept = sem("step_kept")
        scratch_written = sem("scratch_written")
        pairs_loaded = sem("pairs_loaded")
        layer_ready = sem("layer_ready")
        layer_kept = sem("layer_kept")
        half_weighted = sem("half_weighted")
        weighted_made = sem("weighted_made")
        out_written = sem("out_written")

        CHUNK_BATCHES = TILES * BATCHES
        CHUNK_STEPS = TILES * STEPS
        assert CHUNK_BATCHES % 2 == CHUNK_STEPS % 2 == HOT_BATCHES % 2 == 0
        SCRATCH_DMAS = 2 * QUADS
        WEIGHTS = 7
        CONSTANTS = 4
        HOT_ID_FIELDS = slice(0, HOT_FIELDS), slice(HOT_FIELDS, len(ONE_HOT))

        assert TRANSPOSED % BATCH_VECTORS and CHUNKS % 2 == 0

        def chunks(engine, chunk):
            chunk(0, True, False, False)
            with engine.Fori(0, CHUNKS // 2 - 1) as pair:
                c = engine.snap(pair * 2 + 1)
                chunk(c, False, False, False)
                c = engine.snap(pair * 2 + 2)
                chunk(c, False, False, True)
            chunk(CHUNKS - 1, False, True, False)

        block = ctx.enter_context(nc.Block())

        @block.sync
        def _(sp):
            def load_dense(c):
                sp.dma_start(dense_sb[:, :], dense[bass.ds(c * DIM, DIM), :]).then_inc(dense_loaded, 16)

            def load_table(n):
                sp.dma_start(stage[n][0:PART_ROWS, :, :],
                             tables[ONE_HOT[n]].rearrange("(p k) d -> p k d", k=PARTS))\
                    .then_inc(table_loaded[n], 16)

            def load_hot_ids(c, n):
                fields = HOT_ID_FIELDS[n]
                width = (fields.stop - fields.start) * CHUNK
                sp.dma_start(hot_ids[:, fields, :].rearrange("p f s -> p (f s)"),
                             ids_of_field[bass.ds(c, 1), fields.start * CHUNK:fields.stop * CHUNK]
                             .broadcast_to([128, width])).then_inc(hot_ids_loaded[n], 16)

            def store_y(at):
                sp.dma_start(out[bass.ds(at, CHUNK), :].rearrange("b o -> o b"), y_sb[:, :]).then_inc(out_written, 16)

            for n, tiles in enumerate((slice(0, TILES), slice(TILES, BATCH // TILE))):
                sp.dma_start(ids_sb[:, tiles, :],
                             ids[tiles.start * TILE:tiles.stop * TILE, :].rearrange("(t p) f -> p t f", p=TILE))\
                    .then_inc(ids_loaded[n], 16)
                if n == 0:
                    load_hot_ids(0, 0)
                    load_table(0)
                    load_hot_ids(0, 1)
                    load_table(1)
            sp.sem_inc(out_written, 16)
            for n in range(2, len(ONE_HOT)):
                load_table(n)
            load_dense(0)
            sp.wait_ge(low_made, HOT_BUFFERS + 1)
            for into, source in (
                (w1_sb[0:PAIR_ROWS, 0:PAIR_TILES, :], w1[0:PAIRS, :].rearrange("(k p) n -> p k n", p=PAIR_ROWS)),
                (w1_sb[:, PAIR_TILES, :], w1[PAIRS:PAIRS + DIM, :]),
                (w1_again, w1[PAIRS + DIM:PAIRS + 2 * DIM, :]),
                (w2_sb[:, :, :], w2.rearrange("(k p) n -> p k n", p=128)),
                (w3_sb[:, :], w3),
                (b1_sb[:, :], b1),
                (b2_sb[:, :], b2),
            ):
                sp.dma_start(into, source).then_inc(weights_loaded, 16)

            def chunk(c, first, last, swing):
                if not last:
                    following = c + 1 if first else sp.snap(c + 1)
                    if first:
                        sp.wait_ge(one_hot_made, len(ONE_HOT))
                    else:
                        sp.wait_ge(batch_ready, c * CHUNK_BATCHES + BATCHES)
                    for n in range(2):
                        load_hot_ids(following, n)
                if not (first or last):
                    at = sp.snap(c * CHUNK - CHUNK)
                    sp.wait_ge(layer_kept, c * LAYER)
                    store_y(at)
                if not last:
                    following = c + 1 if first else sp.snap(c + 1)
                    sp.wait_ge(dense_kept, c + 1)
                    load_dense(following)
                if not first:
                    sp.wait_ge(pairs_loaded, c * 16)
                sp.wait_ge(step_kept, c * CHUNK_STEPS + (2 + CHUNK_STEPS))
                for q in range(QUADS):
                    block_row, block_column = VECTORS * q, VECTORS * (QUADS - 1 - q)
                    for lines, columns, slot in (
                        ((0, VECTORS - 1), (0, VECTORS - 1), VECTORS * (WRAP - VECTORS + 1)),
                        ((DELTAS + 1, VECTORS), (VECTORS - DELTAS, VECTORS), (VECTORS + 1) * (DELTAS + 1)),
                    ):
                        height, width = lines[1] - lines[0], columns[1] - columns[0]
                        into = bass.AP(scratch.tensor, slot * SLOT + q * CHUNK_GROUPS,
                                       [[(VECTORS + 1) * SLOT, height], [VECTORS * SLOT, width], [1, CHUNK_GROUPS]])
                        sp.dma_start(into, products[block_row + lines[0]:block_row + lines[1],
                                                    block_column + columns[0]:block_column + columns[1], :])\
                            .then_inc(scratch_written, 16)
                if last:
                    sp.wait_ge(layer_ready, c * LAYER + (2 - LAYER))
                sp.wait_ge(scratch_written, c * (16 * SCRATCH_DMAS) + 16 * SCRATCH_DMAS)
                sp.dma_start(features[0:PAIR_ROWS, 0:PAIR_TILES, :],
                             scratch[FIRST_SLOT:FIRST_SLOT + PAIRS, :, :]
                             .rearrange("(k p) q g -> p k (q g)", p=PAIR_ROWS)).then_inc(pairs_loaded, 16)

            chunks(sp, chunk)
            for c in (CHUNKS - 2, CHUNKS - 1):
                sp.wait_ge(layer_kept, LAYER * (c + 1))
                store_y(c * CHUNK)
            sp.wait_ge(out_written, 16 * (CHUNKS + 1))

        @block.gpsimd
        def _(pool):
            nc.gpsimd.memset(identity[:, :], 0.0).then_inc(constants_made, 1)
            nc.gpsimd.iota(row_of_int[:, :], pattern=[[1, 1]], base=0, channel_multiplier=PARTS)\
                .then_inc(constants_made, 1)
            nc.gpsimd.memset(ones[:, :], 1.0).then_inc(constants_made, 1)
            pool.wait_ge(constants_made, CONSTANTS - 1)
            nc.gpsimd.affine_select(out=identity[:, :], in_=identity[:, :], compare_op=ALU.not_equal, fill=1.0,
                                    base=0, pattern=[[-1, 128]], channel_multiplier=1).then_inc(constants_made, 1)

            def gather(t, b, swing):
                for v in batch_vectors(b, swing):
                    f = (GATHERED + [SWING])[v]
                    pool.indirect_dma_start(
                        rows[t][:, v, :], None, tables[f][:, :],
                        bass.IndirectOffsetOnAxis(ap=index[t][:, f:f + 1], axis=0),
                    ).then_inc(swing_loaded[t] if f == SWING else rows_loaded[t][b], 16)

            for t in range(TILES):
                pool.wait_ge(index_ready[t], 1)
                for b in range(BATCHES):
                    gather(t, b, False)
            batches = pool.alloc_register("batches")
            pool.reg_mov(batches, 1)

            def chunk(c, last, swing):
                for t in range(TILES):
                    for b in range(BATCHES):
                        count = (c - 1) * CHUNK_BATCHES + t * BATCHES + b + 1 if last else pool.snap(batches)
                        if b == 0:
                            pool.wait_ge(index_ready[t], c + 1)
                        pool.wait_ge(batch_ready, count)
                        if not last:
                            pool.reg_add(batches, batches, 1)
                        gather(t, b, swing)

            with pool.Fori(0, CHUNKS // 2 - 1) as pair:
                c = pool.snap(pair * 2 + 1)
                chunk(c, False, False)
                c = pool.snap(pair * 2 + 2)
                chunk(c, False, True)
            chunk(CHUNKS - 1, True, False)

        @block.tensor
        def _(pe):
            def transpose_batch(c, t, b, swing):
                n = t * BATCHES + b
                batch = batch_vectors(b, swing)
                gathers = len(batch_vectors(b, False))
                pe.wait_ge(rows_loaded[t][b], c * (16 * gathers) + 16 * gathers)
                if len(batch) > gathers:
                    pe.wait_ge(swing_loaded[t], c * 8)
                pe.wait_ge(batch_kept, c * CHUNK_BATCHES + (n + 1))
                for m, v in enumerate(batch):
                    last = nc.tensor.transpose(moved[:, n % 2, m * TILE:(m + 1) * TILE], rows[t][:, v, :],
                                               identity[:, :])
                last.then_inc(batch_ready, 1)

            def multiply(c, t, between=lambda s: None):
                between(0)
                pe.wait_ge(batch_kept, c * CHUNK_BATCHES + (2 + (t + 1) * BATCHES))
                if t == 0:
                    pe.wait_ge(hot_kept, c * HOT_BATCHES + (2 + HOT_BATCHES))
                for s in range(STEPS):
                    n = t * STEPS + s
                    pe.wait_ge(step_kept, c * CHUNK_STEPS + (n + 1))
                    for g in range(STEP_GROUPS):
                        at = t * TILE + (s * STEP_GROUPS + g) * QUADS
                        bank, col = divmod(g, BANK_GROUPS)
                        four = vectors[:, at:at + QUADS, :].rearrange("d s v -> d (s v)")
                        last = nc.tensor.matmul(gram[0:PRODUCT, n % 2, bank, col * PRODUCT:(col + 1) * PRODUCT],
                                                four, four, start=True, stop=True)
                    last.then_inc(step_ready, 1)
                    between(s + 1)

            def look_up(c, h, first_chunk, swing):
                j, m = divmod(h, HOT_FIELDS)
                if first_chunk:
                    pe.wait_ge(high_made, h + 1)
                if m == 0 or h == swing:
                    pe.wait_ge(hot_kept, c * HOT_BATCHES + (j + 1))
                pe.wait_ge(one_hot_made, c * len(ONE_HOT) + (h + 1))
                for part in (high, low):
                    if first_chunk and part is low:
                        pe.wait_ge(low_made, h + 1)
                    for k in range(PARTS):
                        last = nc.tensor.matmul(mlp[:, j % 2, m, :], part[:, h, k, :],
                                                one_hot[:, h % HOT_BUFFERS, k, :],
                                                start=(part is high and k == 0),
                                                stop=(part is low and k == PARTS - 1))
                if m == HOT_FIELDS - 1:
                    last.then_inc(hot_ready, 1)

            def layers(c, between, lookups):
                pe.wait_ge(pairs_loaded, c * 16 + 16)
                pe.wait_ge(dense_kept, c + 1)
                for m in range(MTILES1):
                    if m % 2 == 0 and lookups is None:
                        pe.wait_ge(layer_kept, c * LAYER - 2 + m)
                    if m % 2 == 0 and lookups is not None:
                        pe.wait_ge(hot_kept, lookups * HOT_BATCHES + (2 + HOT_BATCHES - 1 + m // 2))
                    for k in range(KTILES):
                        height = PAIR_ROWS if k < PAIR_TILES else DIM
                        last = nc.tensor.matmul(mlp[:, m // 2, m % 2, :],
                                                w1_sb[0:height, k, m * 128:(m + 1) * 128],
                                                features[0:height, k, :], start=(k == 0), stop=(k == KTILES - 1))
                    if m % 2:
                        last.then_inc(layer_ready, 1)
                    between(m)
                for m in range(MTILES2):
                    for k in range(MTILES1):
                        if m == 0 and k % 2 == 0:
                            pe.wait_ge(layer_kept, c * LAYER + (1 + k // 2))
                        last = nc.tensor.matmul(mlp[:, m, 0, :], w2_sb[:, k, m * 128:(m + 1) * 128],
                                                hidden1[:, k, :], start=(k == 0), stop=(k == MTILES1 - 1))
                    last.then_inc(layer_ready, 1)
                between(4)

            def last_layer(c):
                pe.wait_ge(weighted_made, c + 1)
                nc.tensor.matmul(mlp[0:1, 1, 1, :], ones[:, :], weighted[:, :], start=True, stop=True)\
                    .then_inc(layer_ready, 1)

            def chunk(c, first, last, swing):
                after = TILE0_AFTER_FIRST if first else TILE0_AFTER
                for h in range(0 if first else EARLY, len(ONE_HOT)):
                    look_up(c, h, first, swing)
                    if h in after:
                        transpose_batch(c, 0, after.index(h), swing)
                if not (first or last):
                    layers(c - 1, lambda n: [transpose_batch(c, 1, b, swing) for b in IN_LAYERS[n]], c)
                in_products = IN_FIRST_PRODUCTS if first else IN_LAST_PRODUCTS if last else IN_PRODUCTS
                multiply(c, 0, lambda s: [transpose_batch(c, 1, b, swing) for b in in_products[s]])
                if not (first or last):
                    last_layer(c - 1)
                if not last:
                    following_swing = not (first or swing)
                    for h in range(following_swing, EARLY):
                        look_up(c + 1, h, False, following_swing)
                    if first:
                        for b in LATE_FIRST:
                            transpose_batch(c, 1, b, swing)
                multiply(c, 1)
                if first:
                    pe.wait_ge(weights_summed, 1)
                if last:
                    layers(c - 1, lambda n: None, None)

            pe.wait_ge(constants_made, CONSTANTS)
            chunks(pe, chunk)
            layers(CHUNKS - 1, lambda n: last_layer(CHUNKS - 2) if n == 0 else None, None)
            last_layer(CHUNKS - 1)

        @block.vector
        def _(dve):
            def ready_index(tile, t):
                nc.vector.tensor_copy(index[t][:, :], ids_sb[:, tile, :]).then_inc(index_ready[t], 1)

            def shift_hot_ids(fields):
                nc.vector.tensor_scalar(hot_ids[:, fields, :], hot_ids[:, fields, :], row_of[:, 0:1], None,
                                        ALU.subtract).then_inc(hot_ids_shifted, 1)

            def make_one_hots(h, swing=False):
                skipped = int(swing and h == 0)
                buffer = h % HOT_BUFFERS
                for k in range(PARTS):
                    last = nc.vector.tensor_scalar(one_hot[:, buffer + skipped:buffer + HOT_FIELDS, k, :],
                                                   hot_ids[0:PART_ROWS, h + skipped:h + HOT_FIELDS, :], float(k), None,
                                                   ALU.is_equal)
                last.then_inc(one_hot_made, HOT_FIELDS)

            def keep_lookups(c, first, swing, and_then):
                made = HOT_BUFFERS
                for j in range(HOT_BATCHES):
                    if j == HOT_BATCHES - 1:
                        and_then()
                    if j == 0 and not first:
                        dve.wait_ge(step_ready, c * CHUNK_STEPS)
                    dve.wait_ge(hot_ready, c * HOT_BATCHES + (j + 1))
                    v = TRANSPOSED + j * HOT_FIELDS
                    skipped = int(swing and j == 0)
                    nc.vector.tensor_copy(vectors[:, :, v + skipped:v + HOT_FIELDS].rearrange("d s v -> d v s"),
                                          mlp[:, j % 2, skipped:HOT_FIELDS, :]).then_inc(hot_kept, 1)
                    if made < len(ONE_HOT):
                        make_one_hots(made)
                        for h in range(made, made + HOT_FIELDS):
                            if first:
                                split(h)
                        made += HOT_FIELDS
                    if j == 0:
                        dve.wait_ge(dense_loaded, c * 16 + 16)
                        nc.vector.tensor_copy(vectors[:, :, DENSE], dense_sb[:, :])

            def split(h):
                dve.wait_ge(high_made, h + 1)
                nc.vector.tensor_tensor(low[:, h, :, :], stage[h][0:PART_ROWS, :, :],
                                        high[:, h, :, :].bitcast(fp32), ALU.subtract).then_inc(low_made, 1)

            def weigh(c):
                dve.wait_ge(layer_kept, c * LAYER + 3)
                nc.vector.tensor_scalar(weighted[:, :], hidden2[:, 0, :], w3_sb[:, 0:1], None, ALU.mult)\
                    .then_inc(half_weighted, 1)
                dve.wait_ge(half_weighted, c + 1)
                dve.wait_ge(layer_kept, c * LAYER + 4)
                nc.vector.scalar_tensor_tensor(weighted[:, :], hidden2[:, 1, :], w3_sb[:, 1:2], weighted[:, :],
                                               ALU.mult, ALU.add).then_inc(weighted_made, 1)

            dve.sem_inc(hot_kept, 2)
            dve.wait_ge(ids_loaded[0], 16)
            for t in range(TILES):
                ready_index(t, t)
            dve.wait_ge(constants_made, CONSTANTS)
            nc.vector.tensor_copy(row_of[:, :], row_of_int[:, :]).then_inc(rows_numbered, 1)
            dve.wait_ge(rows_numbered, 1)
            for h in range(0, HOT_BUFFERS, HOT_FIELDS):
                n = h // HOT_FIELDS
                dve.wait_ge(hot_ids_loaded[n], 16)
                shift_hot_ids(HOT_ID_FIELDS[n])
                dve.wait_ge(hot_ids_shifted, n + 1)
                make_one_hots(h)
                split(h)
                split(h + 1)

            def chunk(c, first, last, swing):
                tile = c * TILES + TILES
                if not first:
                    tile = dve.snap(tile)

                def next_index(t):
                    if not last:
                        dve.wait_ge(batch_ready, c * CHUNK_BATCHES + (t + 1) * BATCHES)
                        if first and t == 0:
                            dve.wait_ge(ids_loaded[1], 16)
                        ready_index(bass.ds(tile + t, 1), t)

                keep_lookups(c, first, swing, lambda: next_index(0))
                if first:
                    dve.wait_ge(weights_loaded, 16 * WEIGHTS)
                    nc.vector.tensor_tensor(w1_sb[:, PAIR_TILES, :], w1_sb[:, PAIR_TILES, :], w1_again[:, :],
                                            ALU.add).then_inc(weights_summed, 1)
                if not (first or last):
                    weigh(c - 1)
                if not last:
                    for n in range(2):
                        dve.wait_ge(hot_ids_loaded[n], c * 16 + 32)
                    shift_hot_ids(slice(0, len(ONE_HOT)))
                    dve.wait_ge(hot_ids_shifted, c + 3)
                    for h in range(0, HOT_BUFFERS, HOT_FIELDS):
                        make_one_hots(h, swing=not (first or swing))
                next_index(1)
                if not first:
                    dve.wait_ge(layer_ready, c * LAYER + (2 - LAYER))
                nc.vector.tensor_copy(features[:, PAIR_TILES, :].rearrange("d (q g) -> d q g", q=QUADS),
                                      dense_sb[:, :].rearrange("d (g q) -> d q g", q=QUADS)).then_inc(dense_kept, 1)

            chunks(dve, chunk)
            for c in (CHUNKS - 2, CHUNKS - 1):
                weigh(c)

        @block.scalar
        def _(act):
            act.sem_inc(batch_kept, 2)
            act.sem_inc(step_kept, 2)

            def keep_batch(c, t, b, swing):
                n = t * BATCHES + b
                batch = batch_vectors(b, swing)
                act.wait_ge(batch_ready, c * CHUNK_BATCHES + (n + 1))
                nc.scalar.activation(
                    vectors[:, t * TILE:(t + 1) * TILE, batch[0]:batch[-1] + 1].rearrange("d s v -> d v s"),
                    moved[:, n % 2, 0:len(batch) * TILE].rearrange("d (v s) -> d v s", s=TILE), ACT.Copy)\
                    .then_inc(batch_kept, 1)

            def keep_products(c, t, between=lambda s: None):
                between(0)
                for s in range(STEPS):
                    n = t * STEPS + s
                    first = t * GROUPS + s * STEP_GROUPS
                    act.wait_ge(step_ready, c * CHUNK_STEPS + (n + 1))
                    nc.scalar.activation(
                        products[0:PRODUCT, ::-1, first:first + STEP_GROUPS].rearrange("p x (b g) -> p b g x", b=2),
                        gram[0:PRODUCT, n % 2, :, 0:BANK_GROUPS * PRODUCT]
                        .rearrange("p b (g x) -> p b g x", g=BANK_GROUPS), ACT.Copy).then_inc(step_kept, 1)
                    between(s + 1)

            def keep_layers(c, between=lambda n: None):
                between(0)
                for half in range(2):
                    act.wait_ge(layer_ready, c * LAYER + (half + 1))
                    for m in range(2 * half, 2 * half + 2):
                        last = nc.scalar.activation(hidden1[:, m, :], mlp[:, half, m % 2, :], ACT.Relu,
                                                    bias=b1_sb[:, m:m + 1])
                    last.then_inc(layer_kept, 1)
                    if half == 0:
                        between(1)
                        between(2)
                between(3)
                for m in range(MTILES2):
                    act.wait_ge(layer_ready, c * LAYER + (3 + m))
                    nc.scalar.activation(hidden2[:, m, :], mlp[:, m, 0, :], ACT.Relu, bias=b2_sb[:, m:m + 1])\
                        .then_inc(layer_kept, 1)
                between(4)

            def keep_y(c):
                act.wait_ge(layer_ready, c * LAYER + 5)
                act.wait_ge(out_written, c * 16 + 16)
                nc.scalar.activation(
                    y_sb[:, :].rearrange("o (g q) -> o q g", q=QUADS),
                    mlp[0:1, 1, 1, :].rearrange("o (q g) -> o q g", q=QUADS), ACT.Copy).then_inc(layer_kept, 1)

            def chunk(c, first, last, swing):
                for b in range(BATCHES):
                    keep_batch(c, 0, b, swing)
                if not (first or last):
                    keep_layers(c - 1, lambda n: [keep_batch(c, 1, b, swing) for b in IN_LAYERS[n]])
                if not first:
                    act.wait_ge(scratch_written, c * (16 * SCRATCH_DMAS))
                in_products = IN_FIRST_PRODUCTS if first else IN_LAST_PRODUCTS if last else IN_PRODUCTS
                keep_products(c, 0, lambda s: [keep_batch(c, 1, b, swing) for b in in_products[s]])
                if first:
                    for b in LATE_FIRST:
                        keep_batch(c, 1, b, swing)
                if not (first or last):
                    keep_y(c - 1)
                keep_products(c, 1)
                if first:
                    act.wait_ge(weights_loaded, 16 * WEIGHTS)
                if last:
                    keep_layers(c - 1)
                    keep_y(c - 1)

            for h in range(len(ONE_HOT)):
                act.wait_ge(table_loaded[h], 16)
                nc.scalar.activation(high[:, h, :, :], stage[h][0:PART_ROWS, :, :], ACT.Copy).then_inc(high_made, 1)
            chunks(act, chunk)
            keep_layers(CHUNKS - 1)
            keep_y(CHUNKS - 1)


def _w1_order():
    at = {}
    for a in range(VECTORS):
        for b in range(a + 1, VECTORS):
            at[a, b] = DIM + len(at)
    reference = [f + 1 for f in GATHERED + ONE_HOT] + [0]
    order = []
    for delta in range(DELTAS, 0, -1):
        for i in range(VECTORS):
            a, b = reference[i], reference[(i + delta) % VECTORS]
            order.append(at[min(a, b), max(a, b)])
    return order + list(range(DIM)) + list(range(DIM + PAIRS, DIM + PAIRS + DIM))


def kernel(**inputs):
    import numpy as _np
    import concourse.bacc as _bacc
    from concourse import mybir as _mybir
    from concourse.bass_utils import run_bass_kernel_spmd as _run

    nc = _bacc.Bacc("TRN2", target_bir_lowering=False, num_devices=1)
    arrays = {}

    def declare(name, a):
        arrays[f"in_{name}_dram"] = _np.ascontiguousarray(a)
        return nc.dram_tensor(f"in_{name}_dram", a.shape, _mybir.dt.from_np(a.dtype), kind="ExternalInput").ap()

    def chunk_by_chunk(a):
        return a.reshape(CHUNKS, CHUNK, -1).transpose(0, 2, 1)

    dense = declare("dense", chunk_by_chunk(_np.asarray(inputs["r_dense_features"])).reshape(CHUNKS * DIM, CHUNK))
    ids = declare("ids", inputs["ids"])
    ids_of_field = declare("ids_of_field",
                           chunk_by_chunk(_np.asarray(inputs["ids"])[:, ONE_HOT]).reshape(CHUNKS, -1))
    tables = [declare(f"tbl_{f}", inputs[f"tbl_{f}"]) for f in range(FIELDS)]
    w1 = declare("w1", _np.asarray(inputs["W_top1"])[_w1_order()])

    def columns(name):
        return declare(name, _np.asarray(inputs[name]).reshape(-1, 128).T)

    rest = [columns("b_top1"), declare("W_top2", inputs["W_top2"]), columns("b_top2"), columns("W_top3")]
    out = nc.dram_tensor("out_0_dram", (BATCH, 1), _mybir.dt.float32, kind="ExternalOutput").ap()
    build(nc, dense, ids, ids_of_field, tables, w1, *rest, out)
    r = _run(nc, [arrays], core_ids=[0])
    return r.results[0]["out_0_dram"]
```
